# Optimizing a Trainium2 kernel written in Bass

```python
import numpy as np
import jax
import jax.numpy as jnp

def _softmax(x, axis=-1):
    return jax.nn.softmax(x, axis=axis)

def _gelu(x):
    return jax.nn.gelu(x, approximate=True)

def _silu(x):
    return jax.nn.silu(x)

def _sigmoid(x):
    return jax.nn.sigmoid(x)

def _layernorm(x, axis=-1, eps=1e-05):
    m = jnp.mean(x, axis=axis, keepdims=True)
    v = jnp.var(x, axis=axis, keepdims=True)
    return (x - m) / jnp.sqrt(v + eps)

def _scatter_add(tgt, idx, src, axis=0):
    return tgt.at[idx].add(src)

def _segment_sum(src, seg, n):
    return jax.ops.segment_sum(src, seg, n)
kernel_name = 'mk_seq_preln_d1_jaxref_r4_d279df'

def setup_inputs(seed: int=0):
    np.random.seed(seed)
    _w = jnp.asarray

    def _L0_attn_setup():
        import jax, jax.numpy as jnp
        import numpy as np
        N_HEADS = 16

        def _rope_tables(C, d_head):
            i = jnp.arange(d_head // 2, dtype=jnp.float32)
            theta = jnp.power(10000.0, -2.0 * (i - 1.0) / d_head)
            ang = jnp.arange(C, dtype=jnp.float32)[:, None] * theta[None, :]
            return (jnp.cos(ang), jnp.sin(ang))

        def _rotate(t, cos, sin):
            te, to = (t[..., 0::2], t[..., 1::2])
            re = te * cos - to * sin
            ro = te * sin + to * cos
            return jnp.stack([re, ro], axis=-1).reshape(t.shape)
        key = jax.random.key(seed)
        k1, k2, k3 = jax.random.split(key, 3)
        B, C, D = (2, 512, 256)
        x = jax.random.normal(k1, (B, C, D), dtype=jnp.float32)
        Wqkv = jax.random.normal(k2, (D, 3 * D), dtype=jnp.float32) * 0.02
        Wout = jax.random.normal(k3, (D, D), dtype=jnp.float32) * 0.02
        bout = jnp.zeros((D,), dtype=jnp.float32)
        return {'x': x, 'Wqkv': Wqkv, 'Wout': Wout, 'bout': bout}
    _L0_attn_in = _L0_attn_setup()

    def _L0_ffn_setup():
        import jax, jax.numpy as jnp
        import numpy as np
        D_MODEL = 256
        EXPERT_DIM = 128
        N_EXPERTS = 8
        TOP_K = 2

        def _sq_relu(h):
            return jnp.square(jax.nn.relu(h))
        key = jax.random.key(seed)
        ks = jax.random.split(key, 6)
        s = 0.02
        x = jax.random.normal(ks[0], (2, 512, D_MODEL), dtype=jnp.float32)
        Ws1 = jax.random.normal(ks[1], (D_MODEL, EXPERT_DIM), dtype=jnp.float32) * s
        Ws2 = jax.random.normal(ks[2], (EXPERT_DIM, D_MODEL), dtype=jnp.float32) * s
        W1 = jax.random.normal(ks[3], (N_EXPERTS, D_MODEL, EXPERT_DIM), dtype=jnp.float32) * s
        W2 = jax.random.normal(ks[4], (N_EXPERTS, EXPERT_DIM, D_MODEL), dtype=jnp.float32) * s
        Wr = jax.random.normal(ks[5], (D_MODEL, N_EXPERTS), dtype=jnp.float32) * s
        return {'x': x, 'Ws1': Ws1, 'Ws2': Ws2, 'W1': W1, 'W2': W2, 'Wr': Wr}
    _L0_ffn_in = _L0_ffn_setup()
    _d = {'L0_attn_x': _L0_attn_in['x'], 'L0_attn_Wqkv': _L0_attn_in['Wqkv'], 'L0_attn_Wout': _L0_attn_in['Wout'], 'L0_attn_bout': _L0_attn_in['bout'], 'L0_ffn_Ws1': _L0_ffn_in['Ws1'], 'L0_ffn_Ws2': _L0_ffn_in['Ws2'], 'L0_ffn_W1': _L0_ffn_in['W1'], 'L0_ffn_W2': _L0_ffn_in['W2'], 'L0_ffn_Wr': _L0_ffn_in['Wr']}
    _x0 = _d['L0_attn_x']
    _d['L0_attn_x'] = jax.random.normal(jax.random.fold_in(jax.random.key(seed), 1), (8, 1024, 256), dtype=_x0.dtype)
    del _x0
    return _d

def reference(L0_attn_x, L0_attn_Wqkv, L0_attn_Wout, L0_attn_bout, L0_ffn_Ws1, L0_ffn_Ws2, L0_ffn_W1, L0_ffn_W2, L0_ffn_Wr):

    def _L0_attn_ref(x, Wqkv, Wout, bout):
        import jax, jax.numpy as jnp
        import numpy as np
        N_HEADS = 16

        def _rope_tables(C, d_head):
            i = jnp.arange(d_head // 2, dtype=jnp.float32)
            theta = jnp.power(10000.0, -2.0 * (i - 1.0) / d_head)
            ang = jnp.arange(C, dtype=jnp.float32)[:, None] * theta[None, :]
            return (jnp.cos(ang), jnp.sin(ang))

        def _rotate(t, cos, sin):
            te, to = (t[..., 0::2], t[..., 1::2])
            re = te * cos - to * sin
            ro = te * sin + to * cos
            return jnp.stack([re, ro], axis=-1).reshape(t.shape)
        B, C, D = x.shape
        H = N_HEADS
        dh = D // H
        qkv = x @ Wqkv
        q, k, v = jnp.split(qkv, 3, axis=-1)
        q = q.reshape(B, C, H, dh).transpose(0, 2, 1, 3)
        k = k.reshape(B, C, H, dh).transpose(0, 2, 1, 3)
        v = v.reshape(B, C, H, dh).transpose(0, 2, 1, 3)
        cos, sin = _rope_tables(C, dh)
        q_rot = _rotate(q, cos, sin)
        k_rot = _rotate(k, cos, sin)
        scale = 1.0 / jnp.sqrt(jnp.asarray(dh, dtype=x.dtype))
        num = jnp.exp(jnp.einsum('bhqd,bhkd->bhqk', q_rot, k_rot) * scale)
        den = jnp.sum(jnp.exp(jnp.einsum('bhqd,bhkd->bhqk', q, k) * scale), axis=-1, keepdims=True)
        attn = num / den
        causal = jnp.tril(jnp.ones((C, C), dtype=bool))
        attn = jnp.where(causal[None, None], attn, 0.0)
        y = jnp.einsum('bhqk,bhkd->bhqd', attn, v)
        y = y.transpose(0, 2, 1, 3).reshape(B, C, D)
        return y @ Wout + bout

    def _L0_ffn_ref(x, Ws1, Ws2, W1, W2, Wr):
        import jax, jax.numpy as jnp
        import numpy as np
        D_MODEL = 256
        EXPERT_DIM = 128
        N_EXPERTS = 8
        TOP_K = 2

        def _sq_relu(h):
            return jnp.square(jax.nn.relu(h))
        shape = x.shape
        xf = x.reshape(-1, D_MODEL)
        out_shared = _sq_relu(xf @ Ws1) @ Ws2
        logits = xf @ Wr
        top_vals, top_idx = jax.lax.top_k(logits, TOP_K)
        rw = jax.nn.softmax(top_vals.astype(jnp.float32), axis=-1).astype(x.dtype)
        onehot = jax.nn.one_hot(top_idx, N_EXPERTS, dtype=x.dtype)
        prob = jnp.einsum('tk,tke->te', rw, onehot)
        prob = jnp.trunc(prob)
        h = _sq_relu(jnp.einsum('td,edf->tef', xf, W1))
        y = jnp.einsum('tef,efd->ted', h, W2)
        out_routed = jnp.einsum('ted,te->td', y, prob)
        return (out_shared + out_routed).reshape(shape)
    x = L0_attn_x
    x = x + _L0_attn_ref(_layernorm(x, axis=-1), L0_attn_Wqkv, L0_attn_Wout, L0_attn_bout)
    x = x + _L0_ffn_ref(_layernorm(x, axis=-1), L0_ffn_Ws1, L0_ffn_Ws2, L0_ffn_W1, L0_ffn_W2, L0_ffn_Wr)
    return x

_drawn_inputs = setup_inputs


def setup_inputs(seed=0):
    import zlib

    import numpy as np

    out = dict(_drawn_inputs(seed))
    spreads = {'L0_attn_bout': (0.0, 0.1)}
    factors = {}
    for name, (base, spread) in spreads.items():
        noise = np.random.default_rng([zlib.crc32(name.encode()), seed]).standard_normal(out[name].shape)
        drawn = base * np.exp(spread * noise) if base else spread * noise
        out[name] = jnp.asarray(drawn.astype(out[name].dtype))
    for name, factor in factors.items():
        out[name] = (out[name] * factor).astype(out[name].dtype)
    return out
```

```python
import concourse.bass as bass
from concourse import mybir
from contextlib import ExitStack
import numpy as np


F32 = mybir.dt.float32
BF16 = mybir.dt.bfloat16
I32 = mybir.dt.int32
ALU = mybir.AluOpType
ACT = mybir.ActivationFunctionType
AXIS_X = mybir.AxisListType.X

B, C, D = 8, 1024, 256
H, DH = 16, 16
HG = 4
G = H // HG
P = 128
NB = C // P
KC = D // P
E, F = 8, 128
HALF = C // 2
PARTS, TERMS = 3, 6
ROWS = TERMS * DH
EPS = 1e-5
SCALE = 1.0 / DH ** 0.5
RING = 3


CHUNKS = [
    [(0, 0, 0, 512, 512), (1, 0, 1, 512, 512)],
    [(0, 0, 2, 512, 512), (1, 0, 3, 512, 512)],
    [(0, 0, 4, 512, 512), (1, 0, 7, 896, 128), (1, 128, 5, 640, 384)],
    [(0, 0, 0, 0, 512), (1, 0, 6, 768, 256), (1, 256, 2, 256, 256)],
    [(0, 0, 1, 128, 384), (0, 384, 3, 384, 128)],
]
DIAGONALS = {2: [(0, 2, 512), (640, 1, 0)], 3: [(0, 2, 512), (768, 1, 0)], 4: [(0, 2, 384)]}
MASKS = {c: len(d) * HG for c, d in DIAGONALS.items()}
MASKS_UNIT = sum(MASKS.values())


def unit_steps():
    steps, dens = [], [("den", j, i) for j in range(HG) for i in range(NB)]
    for c, count in zip(range(5), (7, 7, 6, 6, 6)):
        steps += [("num", c, j) for j in (range(HG) if c < 4 else range(0, HG, 2))]
        steps += [dens.pop(0) for _ in range(count)]
    return steps


STEPS = unit_steps()
NSTEP = len(STEPS)
LAST_STEP = {c: max(s for s, x in enumerate(STEPS) if x[:2] == ("num", c)) for c in range(5)}
FIRST_DEN = next(s for s, x in enumerate(STEPS) if x[0] == "den")
GATE_STEP = 43

PV_AT = {10: (0, 0), 11: (0, 1), 18: (1, 0), 19: (1, 1), 30: (2, 0), 31: (2, 2), 32: (2, 1),
         40: (3, 1), 42: (3, 0), 43: (3, 2), 48: (4, 0), 49: (4, 1)}
PV_LAST = {11, 19, 32, 43, 49}
Y_FIRST, Y_LAST = {10: 0, 42: 1}, {40, 49}

def side_tiles(g):
    at = {}
    if g == 0:
        at.update({0: ("v", 0), 2: ("v", 1), 4: ("v", 2), 6: ("v", 3)})
    if g == G - 1:
        at.update({0: ("xt", 0), 2: ("xt", 1), 4: ("xt", 2), 6: ("xt", 3)})
    q0 = 8 if g in (0, G - 1) else 0
    at.update({q0 + 4 * i: ("qk", i) for i in range(4)})
    at.update({23: ("norm", 0), 25: ("norm", 1)})
    at.update({27 + 2 * i: ("acc", i) for i in range(4)})
    at.update({35: ("ffn", 0), 37: ("ffn", 1), 39: ("ffn", 2), 45: ("ffn", 3), 47: ("ffn", 4)})
    return at


FFN_TILES = 5
GEN_TILES = 3


def block(nc, x, w_qkv, w_out, b_out, ws1, ws2, w1, w2, wr, cos_in, sin_in, out):
    x_v = x.rearrange("b (n p) d -> b p n d", p=P)
    out_v = out.rearrange("b (n p) d -> b p n d", p=P)
    scratch = nc.dram_tensor("qk_parts", (2, PARTS, 2, DH * HG, C), BF16, kind="Internal").ap()

    with ExitStack() as ctx:
        def sb(name, shape, dt=F32):
            return ctx.enter_context(nc.sbuf_tensor(name, shape, dt))

        def ps(name, shape):
            return ctx.enter_context(nc.psum_tensor(name, shape, F32))

        def sem(name):
            return ctx.enter_context(nc.semaphore(name))

        stack = sb("stack", [P, 2, 2, 2, HG * C], BF16)
        probs = sb("probs", [P, 2, HG, C])
        x_in = sb("x_in", [P, NB, D])
        xn = sb("xn", [P, 2, D])
        xnt = sb("xnt", [P, KC, C])
        v_sb = sb("v_sb", [P, NB, D])
        x_acc = sb("x_acc", [P, NB, D])
        x_mid = sb("x_mid", [P, NB, D])
        y_sb = sb("y_sb", [P, C])
        w_qk = sb("w_qk", [P, KC, G, 2, P])
        w_v = sb("w_v", [P, KC, D])
        w_o = sb("w_o", [P, G, D])
        ws1_sb = sb("ws1_sb", [P, KC, F])
        ws2_sb = sb("ws2_sb", [P, D])
        wr_sb = sb("wr_sb", [P, KC, E])
        w1_sb = sb("w1_sb", [P, KC, E, F])
        w2_sb = sb("w2_sb", [P, E, D])
        cos_sb = sb("cos_sb", [P, C])
        sin_sb = sb("sin_sb", [P, C])
        bias = sb("bias", [P, D])
        ident = sb("ident", [P, P])
        ones = sb("ones", [P, P])
        parts = sb("parts", [P, 2, PARTS, HALF], BF16)
        rest = sb("rest", [P, HALF])
        rot = sb("rot", [P, HALF])
        den = sb("den", [P, 2, NB, HG])
        rden = sb("rden", [P, NB, HG])
        spread = [rest[:, :], rot[:, :]]
        stats = sb("stats", [P, NB, 6])
        mean_var = sb("mean_var", [P, NB + 2, 2])
        rstd = sb("rstd", [P, NB + 2])
        root = [sb(f"root{i}", [P, NB]) for i in range(3)]
        xn2 = sb("xn2", [P, 2, D])
        xn2t = sb("xn2t", [P, KC, 2 * P])
        hidden = sb("hidden", [P, 2 * P])
        hidden2 = sb("hidden2", [P, 2 * P])
        logits = sb("logits", [P, 2, E])
        top = sb("top", [P, 2, 8])
        gap = sb("gap", [P, 2])
        gap_exp = sb("gap_exp", [P, 2])
        weight = sb("weight", [P, 2])
        prob = sb("prob", [P, 2, E])
        routed = sb("routed", [1, 2])
        routed_i = sb("routed_i", [1, 1], I32)
        gate = sb("gate", [P, 2 * P])
        w1_now = sb("w1_now", [P, KC, F])
        w2_now = sb("w2_now", [P, D])
        y_out = sb("y_out", [P, 2, D])

        scores = ps("scores", [P, RING, 2 * HALF])
        y_ps = ps("y_ps", [P, HALF])
        side = ps("side", [P, HALF])

        loaded = sem("loaded")
        consts = sem("consts")
        weights_ready = sem("weights_ready")
        stage_free = sem("stage_free")
        x_loaded = sem("x_loaded")
        plain_sent = sem("plain_sent")
        rot_sent = sem("rot_sent")
        stacked = [sem("stacked0"), sem("stacked1")]
        out_sent = sem("out_sent")
        scores_ready = sem("scores_ready")
        exp_done = sem("exp_done")
        masked = sem("masked")
        chunk_used = sem("chunk_used")
        y_ready = sem("y_ready")
        y_taken = sem("y_taken")
        spread_ready = sem("spread_ready")
        den_used = sem("den_used")
        full = {k: sem(f"{k}_full") for k in ("v", "xt", "qk", "norm", "acc", "ffn", "gen")}
        taken = {k: sem(f"{k}_taken") for k in ("v", "xt", "qk", "norm", "acc", "ffn", "gen")}
        xn_ready = sem("xn_ready")
        xn2_ready = sem("xn2_ready")
        parts_ready = sem("parts_ready")
        gap_ready = sem("gap_ready")
        gap_exped = sem("gap_exped")
        weight_ready = sem("weight_ready")
        hidden_ready = sem("hidden_ready")
        routed_ready = sem("routed_ready")
        gate_ready = sem("gate_ready")
        y_out_ready = sem("y_out_ready")

        program = ctx.enter_context(nc.Block())
        LOADS = 12 + KC + 1

        held = {e: sem(f"held_{e}") for e in ("sp", "pool", "pe", "dve")}

        def at1(b, per, k):
            return b * per + k + 1

        def score_tile(n):
            return scores[:, n % RING, :]

        def at(b, per, k):
            return b * per + k

        stage = probs[:, 0, 0, 0:KC * 2 * D].rearrange("p (k n) -> p k n", k=KC)

        @program.sync
        def _(sp):
            sp.dma_start(stage, w_qkv.rearrange("(k p) n -> p k n", p=P)[:, :, 0:2 * D]).then_inc(loaded, 16)
            sp.dma_start(x_in[:, :, :], x_v[0]).then_inc(x_loaded, 16)
            sp.dma_start(w_v[:, :, :], w_qkv.rearrange("(k p) n -> p k n", p=P)[:, :, 2 * D:3 * D]).then_inc(loaded, 16)
            sp.dma_start(cos_sb[:, :], cos_in).then_inc(loaded, 16)
            sp.dma_start(sin_sb[:, :], sin_in).then_inc(loaded, 16)
            sp.wait_ge(consts, 1)
            wo_v = w_out.rearrange("(g j d) n -> j d g n", j=HG, d=DH)
            for j in range(HG):
                sp.dma_start(w_o[32 * j:32 * j + DH, :, :], wo_v[j]).then_inc(loaded, 16)
            sp.dma_start(bias[:, :], b_out.rearrange("(a n) -> a n", a=1).to_broadcast([P, D])).then_inc(loaded, 16)
            sp.dma_start(ws1_sb[:, :, :], ws1.rearrange("(k p) f -> p k f", p=P)).then_inc(loaded, 16)
            sp.dma_start(ws2_sb[:, :], ws2).then_inc(loaded, 16)
            sp.dma_start(wr_sb[:, :, :], wr.rearrange("(k p) e -> p k e", p=P)).then_inc(loaded, 16)
            for k in range(KC):
                sp.dma_start(w1_sb[:, k, :, :], w1[:, k * P:(k + 1) * P, :].rearrange("e p f -> p e f")).then_inc(loaded, 16)
            sp.dma_start(w2_sb[:, :, :], w2.rearrange("e f d -> f e d")).then_inc(loaded, 16)

            def send_parts(b, g):
                parity = g % 2
                if not (isinstance(b, int) and b == 0 and g == 0):
                    sp.wait_ge(stacked[1 - parity], at(b, 2 * 12 * 16, (g + parity) // 2 * 12 * 16))
                    sp.sem_inc(held["sp"], 1)
                for half in range(2):
                    for kind, sent in ((0, plain_sent), (1, rot_sent)):
                        sp.wait_ge(parts_ready, at(b, 16, 4 * g + 2 * half + kind + 1))
                        sp.sem_inc(held["sp"], 1)
                        sp.dma_start(scratch[kind, :, :, :, half * HALF:(half + 1) * HALF].rearrange("c s r t -> (s r) c t"),
                                     parts[:, kind, :, :]).then_inc(sent, 16)
                if not (isinstance(b, int) and b == 0 and g < 2):
                    sp.wait_ge(scores_ready, at(b, G * NSTEP, (g - 1) * NSTEP))
                    sp.sem_inc(held["sp"], 1)
                for kind, sent in ((0, plain_sent), (1, rot_sent)):
                    sp.wait_ge(sent, at(b, 8 * 16, 2 * 16 * (g + 1)))
                    sp.sem_inc(held["sp"], 1)
                    src = scratch[kind].rearrange("c s (d h) t -> c s d (h t)", h=HG)
                    for side_no, runs in ((0, [(0, 1), (0, 1), (0, 1), (1, 1), (1, 1), (2, 1)]),
                                          (1, [(0, 3), (0, 2), (0, 1)])):
                        row = 0
                        if side_no == 0:
                            for part, copies in ((0, 3), (1, 2), (2, 1)):
                                s = src[part, 0]
                                if copies > 1:
                                    s = s.unsqueeze(0).to_broadcast([copies, DH, HG * C])
                                sp.dma_start(stack[row:row + copies * DH, parity, kind, 0, :], s).then_inc(stacked[parity], 16)
                                row += copies * DH
                        else:
                            for first, n in runs:
                                sp.dma_start(stack[row:row + n * DH, parity, kind, 1, :],
                                             src[0:n, 1]).then_inc(stacked[parity], 16)
                                row += n * DH

            def batch(b, first, last):
                for g in range(G):
                    if g < G - 1:
                        send_parts(b, g + 1)
                    elif not last:
                        send_parts(b + 1, 0)
                    if g == 1 and not last:
                        sp.wait_ge(taken["acc"], at(b, 16, 4))
                        sp.sem_inc(held["sp"], 1)
                        sp.dma_start(x_in[:, :, :], x_v[b + 1]).then_inc(x_loaded, 16)
                    if not first:
                        send_out(b - 1, g)

            def send_out(b, g):
                sp.wait_ge(y_out_ready, at(b, G, g + 1))
                sp.sem_inc(held["sp"], 1)
                sp.dma_start(out_v[b][:, 2 * g:2 * g + 2, :], y_out[:, :, :]).then_inc(out_sent, 16)

            sp.sem_inc(out_sent, 1)
            send_parts(0, 0)
            batch(0, True, False)
            with sp.Fori(1, B - 1) as b:
                batch(b, False, False)
            batch(B - 1, False, True)
            for g in range(G):
                send_out(B - 1, g)
            sp.wait_ge(out_sent, at1(B, 16 * G, 0))

        @program.gpsimd
        def _(pool):
            nc.gpsimd.memset(w_o[:, :, :], 0.0).then_inc(consts, 1)
            nc.gpsimd.memset(ones[:, :], 1.0).then_inc(consts, 1)
            nc.gpsimd.memset(ident[:, :], 0.0).then_inc(consts, 1)
            pool.wait_ge(consts, 3)
            nc.gpsimd.affine_select(out=ident[:, :], in_=ident[:, :], compare_op=ALU.not_equal, fill=1.0, base=0,
                                    pattern=[[-1, P]], channel_multiplier=1).then_inc(consts, 1)

            def batch(b):
                for g in range(G):
                    for c, diagonals in DIAGONALS.items():
                        for j in range(HG):
                            step = LAST_STEP[c] - (HG - 1 - j if c < 4 else 1 - j // 2)
                            pool.wait_ge(exp_done, at(b, G * NSTEP, g * NSTEP + step + 1))
                            pool.sem_inc(held["pool"], 1)
                            for col, n, stride in diagonals:
                                p = probs[:, (5 * g + c) % 2, j, :]
                                if n == 1:
                                    v, pattern = p[:, col:col + P], [[1, P]]
                                else:
                                    v = p[:, col:col + n * stride].rearrange("p (n s) -> p n s", n=n)[:, :, 0:P]
                                    pattern = [[0, n], [1, P]]
                                nc.gpsimd.affine_select(out=v, in_=v, compare_op=ALU.is_ge, fill=0.0, base=0,
                                                        pattern=pattern, channel_multiplier=-1).then_inc(masked, 1)

            batch(0)
            with pool.Fori(1, B) as b:
                batch(b)

        @program.scalar
        def _(act):
            def batch(b, first):
                for g in range(G):
                    for s, step in enumerate(STEPS):
                        act_step(b, first, g, s, step)
                        if s == GATE_STEP and not first:
                            exp_gap(b - 1, g)

            def act_step(b, first, g, s, step):
                n = g * NSTEP + s
                act.wait_ge(scores_ready, at(b, G * NSTEP, n + 1))
                src = score_tile(n)
                if step[0] == "den":
                    _, j, i = step
                    if s == FIRST_DEN and not (first and g < 2):
                        act.wait_ge(den_used, at(b, G, g - 1))
                    nc.scalar.activation(src, src, ACT.Exp, scale=SCALE,
                                         accum_out=den[:, g % 2, i, j:j + 1]).then_inc(exp_done, 1)
                    return
                _, c, j = step
                chunk = 5 * g + c
                if j == 0 and not (first and chunk < 2):
                    act.wait_ge(chunk_used, at(b, 5 * G, chunk - 1))
                if j == 0 and first and chunk < 2:
                    act.wait_ge(stage_free, 1)
                if c < 4:
                    nc.scalar.activation(probs[:, chunk % 2, j, :], src, ACT.Exp, scale=SCALE).then_inc(exp_done, 1)
                else:
                    nc.scalar.activation(probs[:, chunk % 2, j:j + 2, 0:HALF], src.rearrange("p (a n) -> p a n", a=2),
                                         ACT.Exp, scale=SCALE).then_inc(exp_done, 1)

            def exp_gap(b, g):
                act.wait_ge(gap_ready, at(b, G, g + 1))
                nc.scalar.activation(gap_exp[:, :], gap[:, :], ACT.Exp).then_inc(gap_exped, 1)

            batch(0, True)
            with act.Fori(1, B) as b:
                batch(b, False)
            for g in range(G):
                exp_gap(B - 1, g)

        @program.tensor
        def _(pe):
            pe.wait_ge(loaded, 16 * LOADS)
            pe.wait_ge(consts, 4)

            def scores_step(b, first, g, s, step):
                n = g * NSTEP + s
                if n >= RING:
                    pe.wait_ge(exp_done, at(b, G * NSTEP, n - RING + 1))
                elif not first:
                    user = max(m for m in range(G * NSTEP) if m % RING == n)
                    pe.wait_ge(exp_done, at(b - 1, G * NSTEP, user + 1))
                tile = score_tile(n)
                q, k = (stack[0:ROWS, g % 2, 0 if step[0] == "den" else 1, a, :].rearrange("p (h t) -> p h t", h=HG)
                        for a in (0, 1))
                if step[0] == "den":
                    _, j, i = step
                    for half in range(2):
                        mm = nc.tensor.matmul(tile[:, half * HALF:(half + 1) * HALF], q[:, j, i * P:(i + 1) * P],
                                              k[:, j, half * HALF:(half + 1) * HALF], start=True, stop=True)
                else:
                    _, c, j = step
                    for h in ((j,) if c < 4 else (j, j + 1)):
                        for bank, col, i, q0, n in CHUNKS[c]:
                            col += (bank + h - j) * HALF
                            mm = nc.tensor.matmul(tile[:, col:col + n], k[:, h, i * P:(i + 1) * P], q[:, h, q0:q0 + n],
                                                  start=True, stop=True)
                mm.then_inc(scores_ready, 1)

            def heads_step(b, first, g, s):
                c, piece = PV_AT[s]
                bank, col, i, q0, n = CHUNKS[c][piece]
                col += bank * HALF
                if s in Y_FIRST and not (first and g == 0 and s == 10):
                    pe.wait_ge(y_taken, at(b, 2 * G, 2 * g + Y_FIRST[s]))
                if s == 10 and g == 0:
                    pe.wait_ge(taken["v"], at(b, 4, 4))
                if c in MASKS:
                    done = sum(m for k, m in MASKS.items() if k <= c)
                    pe.wait_ge(masked, at(b, G * MASKS_UNIT, g * MASKS_UNIT + done))
                else:
                    pe.wait_ge(exp_done, at(b, G * NSTEP, g * NSTEP + LAST_STEP[c] + 1))
                o0 = q0 % HALF
                for j in range(HG):
                    h = g * HG + j
                    mm = nc.tensor.matmul(y_ps[32 * j:32 * j + DH, o0:o0 + n], v_sb[:, i, h * DH:(h + 1) * DH],
                                          probs[:, (5 * g + c) % 2, j, col:col + n], start=s in Y_FIRST, stop=s in Y_LAST,
                                          tile_position=(0, 32 * j), skip_group_check=True)
                if s in PV_LAST:
                    mm.then_inc(chunk_used, 1)
                elif s in Y_LAST:
                    mm.then_inc(y_ready, 1)

            def v_tile(b, t):
                for i in range(2):
                    for k in range(KC):
                        mm = nc.tensor.matmul(side[:, i * D:(i + 1) * D], xnt[:, k, (2 * t + i) * P:(2 * t + i + 1) * P],
                                              w_v[:, k, :], start=k == 0, stop=k == KC - 1)
                mm.then_inc(full["v"], 1)

            def xt_tile(b, t):
                pe.wait_ge(xn_ready, at(b, 4, t + 1))
                for k in range(KC):
                    for i in range(2):
                        mm = nc.tensor.transpose(side[:, (2 * k + i) * P:(2 * k + i + 1) * P], xn[:, i, k * P:(k + 1) * P],
                                                 ident[:, :])
                mm.then_inc(full["xt"], 1)

            def qk_tile(b, g, t):
                half, swapped = t // 2, t % 2
                if t == 0 and g == 0:
                    pe.wait_ge(taken["xt"], at(b, 4, 4))
                for k in range(KC):
                    mm = nc.tensor.matmul(side[:, :], w_qk[:, k, g, swapped, :], xnt[:, k, half * HALF:(half + 1) * HALF],
                                          start=k == 0, stop=k == KC - 1)
                mm.then_inc(full["qk"], 1)

            def norm_tile(b, g, t):
                pe.wait_ge(spread_ready, at(b, 2 * G, 2 * g + t + 1))
                for i in range(NB // 2):
                    mm = nc.tensor.transpose(side[:, i * P:(i + 1) * P], spread[t][:, i * P:(i + 1) * P], ident[:, :])
                mm.then_inc(full["norm"], 1)

            def acc_tile(b, g, t):
                if t == 0:
                    pe.wait_ge(taken["norm"], at(b, 2 * G, 2 * g + 2))
                for i in range(2):
                    mm = nc.tensor.matmul(side[:, i * D:(i + 1) * D], y_sb[:, (2 * t + i) * P:(2 * t + i + 1) * P],
                                          w_o[:, g, :], start=True, stop=True)
                mm.then_inc(full["acc"], 1)

            def ffn_tile(b, g, t):
                if t == 0:
                    pe.wait_ge(xn2_ready, at(b, G, g + 1))
                    for k in range(KC):
                        for i in range(2):
                            mm = nc.tensor.transpose(side[:, (2 * k + i) * P:(2 * k + i + 1) * P],
                                                     xn2[:, i, k * P:(k + 1) * P], ident[:, :])
                elif t == 1:
                    for i in range(2):
                        for k in range(KC):
                            mm = nc.tensor.matmul(side[:, i * E:(i + 1) * E], xn2t[:, k, i * P:(i + 1) * P], wr_sb[:, k, :],
                                                  start=k == 0, stop=k == KC - 1)
                elif t == 2:
                    for k in range(KC):
                        mm = nc.tensor.matmul(side[:, 0:2 * P], ws1_sb[:, k, :], xn2t[:, k, :], start=k == 0, stop=k == KC - 1)
                elif t == 3:
                    pe.wait_ge(weight_ready, at(b, G, g + 1))
                    mm = nc.tensor.matmul(side[:, 0:2], ones[:, :], weight[:, :], start=True, stop=True)
                else:
                    pe.wait_ge(hidden_ready, at(b, G, g + 1))
                    for i in range(2):
                        mm = nc.tensor.matmul(side[:, i * D:(i + 1) * D], hidden2[:, i * P:(i + 1) * P], ws2_sb[:, :],
                                              start=True, stop=True)
                mm.then_inc(full["ffn"], 1)

            def experts(b, g):
                pe.wait_ge(routed_ready, at(b, G, g + 1))
                pe.sem_inc(held["pe"], 1)
                count = pe.value_load(routed_i[0:1, 0:1], min_val=0, max_val=2 * P)
                base = at1(b, GEN_TILES * E * G, GEN_TILES * E * g)
                with pe.If(count > 0):
                    pe.wait_ge(taken["ffn"], at1(b, FFN_TILES * G, FFN_TILES * (g + 1)))
                    pe.sem_inc(held["pe"], 1)
                    with pe.Fori(0, E) as e:
                        pe.wait_ge(gate_ready, at(b, E * G, E * g + 1) + e)
                        pe.wait_ge(taken["gen"], base + e * GEN_TILES)
                        for i in range(2):
                            mm = nc.tensor.transpose(side[:, i * P:(i + 1) * P], gate[:, i * P:(i + 1) * P], ident[:, :])
                        mm.then_inc(full["gen"], 1)
                        pe.wait_ge(taken["gen"], base + e * GEN_TILES + 1)
                        for k in range(KC):
                            mm = nc.tensor.matmul(side[:, 0:2 * P], w1_now[:, k, :], xn2t[:, k, :], start=k == 0, stop=k == KC - 1)
                        mm.then_inc(full["gen"], 1)
                        pe.wait_ge(taken["gen"], base + e * GEN_TILES + 2)
                        for i in range(2):
                            mm = nc.tensor.matmul(side[:, i * D:(i + 1) * D], hidden[:, i * P:(i + 1) * P], w2_now[:, :],
                                                  start=True, stop=True)
                        mm.then_inc(full["gen"], 1)
                with pe.Else():
                    pe.sem_inc(full["gen"], GEN_TILES * E)

            def side_step(b, first, last, g, s):
                if s not in side_tiles(g):
                    return
                kind, t = side_tiles(g)[s]
                if kind == "xt" and last or kind == "qk" and last and g == G - 1:
                    return
                if first and (kind == "ffn" or g == 0 and kind in ("norm", "acc")):
                    return
                if kind == "v":
                    if t == 0 and not first:
                        pe.wait_ge(taken["ffn"], at1(b - 1, FFN_TILES * G, 0))
                        pe.wait_ge(taken["gen"], at1(b - 1, GEN_TILES * E * G, 0))
                        pe.wait_ge(taken["acc"], at(b - 1, 16, 12))
                        pe.wait_ge(taken["qk"], at(b, 16, 4))
                    else:
                        pe.wait_ge(taken["v"], at(b, 4, t)) if t else pe.wait_ge(taken["qk"], 4)
                    v_tile(b, t)
                elif kind == "xt":
                    if t == 0:
                        pe.wait_ge(taken["acc"], at(b, 16, 8))
                        if not first:
                            pe.wait_ge(taken["ffn"], at1(b - 1, FFN_TILES * G, FFN_TILES * 3))
                            pe.wait_ge(taken["gen"], at1(b - 1, GEN_TILES * E * G, GEN_TILES * E * 3))
                    else:
                        pe.wait_ge(taken["xt"], at(b + 1, 4, t))
                    xt_tile(b + 1, t)
                elif kind == "qk":
                    b1, g1 = (b, g + 1) if g < G - 1 else (b + 1, 0)
                    if t == 0:
                        if g == 0:
                            pe.wait_ge(taken["v"], at(b, 4, 4))
                        elif g < G - 1:
                            pe.wait_ge(taken["acc"], at(b, 16, 4 * (g - 1))) if not (first and g == 1) else None
                            if first and g == 1:
                                pe.wait_ge(taken["qk"], 8)
                            if not first:
                                pe.wait_ge(taken["ffn"], at1(b - 1, FFN_TILES * G, FFN_TILES * g))
                                pe.wait_ge(taken["gen"], at1(b - 1, GEN_TILES * E * G, GEN_TILES * E * g))
                    else:
                        pe.wait_ge(taken["qk"], at(b1, 16, 4 * g1 + t))
                    qk_tile(b1, g1, t)
                elif kind == "norm":
                    b0, g0 = (b, g - 1) if g else (b - 1, G - 1)
                    if t == 0:
                        if last and g == G - 1:
                            pe.wait_ge(taken["ffn"], at1(b - 1, FFN_TILES * G, FFN_TILES * g))
                            pe.wait_ge(taken["gen"], at1(b - 1, GEN_TILES * E * G, GEN_TILES * E * g))
                        else:
                            pe.wait_ge(taken["qk"], at(b, 16, 4 * (g + 2)))
                    else:
                        pe.wait_ge(taken["norm"], at(b0, 2 * G, 2 * g0 + 1))
                    norm_tile(b0, g0, t)
                elif kind == "acc":
                    b0, g0 = (b, g - 1) if g else (b - 1, G - 1)
                    if t:
                        pe.wait_ge(taken["acc"], at(b0, 16, 4 * g0 + t))
                    acc_tile(b0, g0, t)
                else:
                    if t == 0:
                        b0, g0 = (b, g - 1) if g else (b - 1, G - 1)
                        pe.wait_ge(taken["acc"], at(b0, 16, 4 * g0 + 4))
                    else:
                        pe.wait_ge(taken["ffn"], at1(b - 1, FFN_TILES * G, FFN_TILES * g + t))
                    ffn_tile(b - 1, g, t)

            def batch(b, first, last):
                for g in range(G):
                    parity = g % 2
                    pe.wait_ge(stacked[parity], at(b, 2 * 12 * 16, (g // 2 + 1) * 12 * 16))
                    for s, step in enumerate(STEPS):
                        scores_step(b, first, g, s, step)
                        if s in PV_AT:
                            heads_step(b, first, g, s)
                        side_step(b, first, last, g, s)
                    if not first:
                        experts(b - 1, g)

            pe.wait_ge(weights_ready, 1)
            for t in range(4):
                if t:
                    pe.wait_ge(taken["xt"], t)
                xt_tile(0, t)
            for t in range(4):
                if t:
                    pe.wait_ge(taken["qk"], t)
                qk_tile(0, 0, t)
            batch(0, True, False)
            with pe.Fori(1, B - 1) as b:
                batch(b, False, False)
            batch(B - 1, False, True)
            last = B - 1
            pe.wait_ge(taken["ffn"], at1(last, FFN_TILES * G, 0))
            pe.wait_ge(taken["gen"], at1(last, GEN_TILES * E * G, 0))
            for t in range(2):
                if t:
                    pe.wait_ge(taken["norm"], at(last, 2 * G, 2 * G - 1))
                norm_tile(last, G - 1, t)
            for t in range(4):
                if t:
                    pe.wait_ge(taken["acc"], at(last, 16, 12 + t))
                acc_tile(last, G - 1, t)
            pe.wait_ge(taken["acc"], at(last, 16, 16))
            for g in range(G):
                for t in range(FFN_TILES):
                    pe.wait_ge(taken["ffn"], at1(last, FFN_TILES * G, FFN_TILES * g + t))
                    if t == 0:
                        pe.wait_ge(taken["gen"], at1(last, GEN_TILES * E * G, GEN_TILES * E * g))
                    ffn_tile(last, g, t)
                experts(last, g)

        @program.vector
        def _(dve):
            def settle():
                dve.drain()

            def inverse_root(n, var, result):
                v, a, y = (r[:, 0:n] for r in root)
                nc.vector.tensor_scalar(v, var, EPS, None, ALU.add)
                settle()
                nc.vector.tensor_scalar(a.bitcast(I32), v.bitcast(I32), 1, None, ALU.logical_shift_right)
                settle()
                nc.vector.tensor_scalar(y.bitcast(I32), a.bitcast(I32), -1.0, float(0x5f3759df), ALU.mult, ALU.add)
                settle()
                for i in range(3):
                    nc.vector.scalar_tensor_tensor(a, y, -0.5, y, ALU.mult, ALU.mult)
                    settle()
                    nc.vector.tensor_tensor(a, a, v, ALU.mult)
                    settle()
                    nc.vector.scalar_tensor_tensor(result if i == 2 else y, a, 1.5, y, ALU.add, ALU.mult)
                    settle()

            def layernorm_stats(src, blocks, at_block):
                for i in range(blocks):
                    nc.vector.bn_stats(stats[:, i, :], src(i))
                settle()
                for i in range(blocks):
                    nc.vector.bn_aggr(mean_var[:, at_block + i, :], stats[:, i, :])
                settle()
                ends = slice(at_block, at_block + blocks)
                inverse_root(blocks, mean_var[:, ends, 1], rstd[:, ends])

            def layernorm(dst, src, i):
                return nc.vector.tensor_scalar(dst, src, mean_var[:, i, 0:1], rstd[:, i:i + 1], ALU.subtract, ALU.mult)

            def v_tile(b, first, t):
                if t == 0 and not first:
                    dve.wait_ge(chunk_used, at(b, 5 * G, 0))
                dve.wait_ge(full["v"], at(b, 4, t + 1))
                nc.vector.tensor_copy(v_sb[:, 2 * t:2 * t + 2, :], side[:, :].rearrange("p (i d) -> p i d", i=2)
                                      ).then_inc(taken["v"], 1)

            def xt_tile(b, t, very_first):
                if not (very_first and t == 0):
                    dve.wait_ge(full["xt"], at(b, 4, t))
                layernorm(xn[:, 0, :], x_in[:, 2 * t, :], 2 * t)
                layernorm(xn[:, 1, :], x_in[:, 2 * t + 1, :], 2 * t + 1).then_inc(xn_ready, 1)
                dve.wait_ge(full["xt"], at(b, 4, t + 1))
                nc.vector.tensor_copy(xnt[:, :, 2 * t * P:(2 * t + 2) * P], side[:, :].rearrange("p (k n) -> p k n", k=KC)
                                      ).then_inc(taken["xt"], 1)

            def split(kind, src, high_done):
                high, middle, low = (parts[:, kind, i, :] for i in range(PARTS))
                nc.vector.tensor_copy(high, src)
                settle()
                last_read = nc.vector.tensor_tensor(rest[:, :], src, high, ALU.subtract)
                return last_read

            def split_rest(kind):
                high, middle, low = (parts[:, kind, i, :] for i in range(PARTS))
                settle()
                nc.vector.tensor_copy(middle, rest[:, :])
                settle()
                nc.vector.tensor_tensor(low, rest[:, :], middle, ALU.subtract).then_inc(parts_ready, 1)

            def qk_tile(b, g, t, very_first):
                half, swapped = t // 2, t % 2
                cols = slice(half * HALF, (half + 1) * HALF)
                dve.wait_ge(full["qk"], at(b, 16, 4 * g + t + 1))
                if not (very_first and half == 0):
                    dve.wait_ge((plain_sent, rot_sent)[swapped], at(b, 8 * 16, 16 * (2 * g + half)))
                if not swapped:
                    nc.vector.tensor_tensor(rot[:, :], side[:, :], cos_sb[:, cols], ALU.mult)
                    split(0, side[:, :], None).then_inc(taken["qk"], 1)
                    split_rest(0)
                else:
                    nc.vector.tensor_tensor(rest[:, :], side[:, :], sin_sb[:, cols], ALU.mult).then_inc(taken["qk"], 1)
                    settle()
                    nc.vector.tensor_tensor(rot[:, :], rot[:, :], rest[:, :], ALU.add)
                    settle()
                    split(1, rot[:, :], None)
                    split_rest(1)
                settle()

            def reciprocals(b, g):
                dve.wait_ge(exp_done, at(b, G * NSTEP, (g + 1) * NSTEP))
                nc.vector.reciprocal(rden[:, :, :], den[:, g % 2, :, :]).then_inc(den_used, 1)
                settle()
                for t in range(2):
                    blocks = slice((1 - t) * NB // 2, (2 - t) * NB // 2)
                    nc.vector.tensor_copy(spread[t].rearrange("p (i h r) -> p i h r", h=HG, r=32),
                                          rden[:, blocks, :].unsqueeze(3).to_broadcast([P, NB // 2, HG, 32])
                                          ).then_inc(spread_ready, 1)

            def take_y(b, g, t):
                if t == 0:
                    dve.wait_ge(y_ready, at(b, G, g + 1))
                else:
                    dve.wait_ge(chunk_used, at(b, 5 * G, 5 * (g + 1)))
                cols = slice((1 - t) * HALF, (2 - t) * HALF)
                nc.vector.tensor_copy(y_sb[:, cols], y_ps[:, :]).then_inc(y_taken, 1)

            def norm_tile(b, g, t):
                settle()
                dve.wait_ge(full["norm"], at(b, 2 * G, 2 * g + t + 1))
                cols = slice((1 - t) * HALF, (2 - t) * HALF)
                nc.vector.tensor_tensor(y_sb[:, cols], side[:, :], y_sb[:, cols], ALU.mult).then_inc(taken["norm"], 1)

            def acc_tile(b, g, t):
                blocks = slice(2 * t, 2 * t + 2)
                dve.wait_ge(full["acc"], at(b, 16, 4 * g + t + 1))
                src = side[:, :].rearrange("p (i d) -> p i d", i=2)
                into = x_mid if g == G - 1 else x_acc
                nc.vector.tensor_tensor(into[:, blocks, :], src, (x_acc if g else x_in)[:, blocks, :], ALU.add
                                        ).then_inc(taken["acc"], 1)
                settle()
                if g == 0:
                    nc.vector.tensor_tensor(x_acc[:, blocks, :], x_acc[:, blocks, :],
                                            bias[:, :].unsqueeze(1).to_broadcast([P, 2, D]), ALU.add)
                    settle()

            def ffn_prepare(b, g):
                layernorm_stats(lambda i: x_mid[:, 2 * g + i, :], 2, NB)
                layernorm(xn2[:, 0, :], x_mid[:, 2 * g, :], NB)
                layernorm(xn2[:, 1, :], x_mid[:, 2 * g + 1, :], NB + 1).then_inc(xn2_ready, 1)

            def ffn_tile(b, g, t):
                dve.wait_ge(full["ffn"], at(b, FFN_TILES * G, FFN_TILES * g + t + 1))
                if t == 0:
                    nc.vector.tensor_copy(xn2t[:, :, :], side[:, :].rearrange("p (k n) -> p k n", k=KC)
                                          ).then_inc(taken["ffn"], 1)
                elif t == 1:
                    nc.vector.tensor_copy(logits[:, :, :], side[:, 0:2 * E].rearrange("p (i e) -> p i e", i=2)
                                          ).then_inc(taken["ffn"], 1)
                    settle()
                    for i in range(2):
                        nc.vector.max(top[:, i, :], logits[:, i, :])
                    settle()
                    nc.vector.tensor_tensor(gap[:, :], top[:, :, 1], top[:, :, 0], ALU.subtract).then_inc(gap_ready, 1)
                elif t == 2:
                    nc.vector.tensor_scalar(hidden[:, :], side[:, 0:2 * P], 0.0, None, ALU.max).then_inc(taken["ffn"], 1)
                    settle()
                    nc.vector.tensor_tensor(hidden2[:, :], hidden[:, :], hidden[:, :], ALU.mult).then_inc(hidden_ready, 1)
                elif t == 3:
                    nc.vector.tensor_copy(routed[:, :], side[0:1, 0:2]).then_inc(taken["ffn"], 1)
                    settle()
                    nc.vector.tensor_tensor(routed_i[:, :], routed[:, 0:1], routed[:, 1:2], ALU.add).then_inc(routed_ready, 1)
                else:
                    dve.wait_ge(out_sent, at1(b, 16 * G, 16 * g))
                    nc.vector.tensor_tensor(y_out[:, :, :], side[:, :].rearrange("p (i d) -> p i d", i=2),
                                            x_mid[:, 2 * g:2 * g + 2, :], ALU.add).then_inc(taken["ffn"], 1)

            def route(b, g):
                dve.wait_ge(gap_exped, at(b, G, g + 1))
                nc.vector.tensor_scalar(weight[:, :], gap_exp[:, :], 1.0, None, ALU.add)
                settle()
                nc.vector.reciprocal(weight[:, :], weight[:, :])
                settle()
                nc.vector.tensor_scalar(weight[:, :], weight[:, :], 1.0, None, ALU.is_ge).then_inc(weight_ready, 1)

            def experts(b, g):
                dve.wait_ge(routed_ready, at(b, G, g + 1))
                dve.sem_inc(held["dve"], 1)
                count = dve.value_load(routed_i[0:1, 0:1], min_val=0, max_val=2 * P)
                base = at(b, GEN_TILES * E * G, GEN_TILES * E * g)
                with dve.If(count > 0):
                    settle()
                    for i in range(2):
                        nc.vector.tensor_scalar(prob[:, i, :], logits[:, i, :], top[:, i, 0:1], weight[:, i:i + 1],
                                                ALU.is_equal, ALU.mult)
                    settle()
                    with dve.Fori(0, E) as e:
                        nc.vector.tensor_copy(w1_now[:, :, :], w1_sb[:, :, bass.ds(e, 1), :].rearrange("p k e f -> p k (e f)"))
                        nc.vector.tensor_copy(w2_now[:, :], w2_sb[:, bass.ds(e, 1), :].rearrange("p e d -> p (e d)"))
                        for i in range(2):
                            last = nc.vector.tensor_copy(gate[:, i * P:(i + 1) * P],
                                                         prob[:, i, bass.ds(e, 1)].to_broadcast([P, P]))
                        last.then_inc(gate_ready, 1)
                        settle()
                        dve.wait_ge(full["gen"], base + e * GEN_TILES + 1)
                        nc.vector.tensor_copy(gate[:, :], side[:, 0:2 * P]).then_inc(taken["gen"], 1)
                        settle()
                        dve.wait_ge(full["gen"], base + e * GEN_TILES + 2)
                        nc.vector.scalar_tensor_tensor(hidden2[:, :], side[:, 0:2 * P], 0.0, gate[:, :], ALU.max, ALU.mult)
                        settle()
                        nc.vector.tensor_tensor(hidden[:, :], hidden2[:, :], hidden2[:, :], ALU.mult).then_inc(taken["gen"], 1)
                        dve.wait_ge(full["gen"], base + e * GEN_TILES + 3)
                        nc.vector.tensor_tensor(y_out[:, :, :], side[:, :].rearrange("p (i d) -> p i d", i=2),
                                                y_out[:, :, :], ALU.add).then_inc(taken["gen"], 1)
                        settle()
                with dve.Else():
                    dve.sem_inc(taken["gen"], GEN_TILES * E)
                    dve.sem_inc(gate_ready, E)
                dve.drain().then_inc(y_out_ready, 1)

            def batch(b, first, last):
                for g in range(G):
                    b0, g0 = (b, g - 1) if g else (b - 1, G - 1)
                    for s in range(NSTEP):
                        if s == 22 and not (first and g == 0):
                            reciprocals(b0, g0)
                        if s == 34 and not first:
                            settle()
                            ffn_prepare(b - 1, g)
                        if s == 48 and g == 2 and not last:
                            dve.wait_ge(x_loaded, at(b, 16, 32))
                            layernorm_stats(lambda i: x_in[:, i, :], NB, 0)
                        if s == 41:
                            take_y(b, g, 0)
                        if s == 42 and not first:
                            route(b - 1, g)
                        if s in side_tiles(g):
                            kind, t = side_tiles(g)[s]
                            if kind == "v":
                                v_tile(b, first, t)
                            elif kind == "xt" and not last:
                                xt_tile(b + 1, t, False)
                            elif kind == "qk" and not (last and g == G - 1):
                                b1, g1 = (b, g + 1) if g < G - 1 else (b + 1, 0)
                                qk_tile(b1, g1, t, False)
                            elif kind == "norm" and not (first and g == 0):
                                norm_tile(b0, g0, t)
                            elif kind == "acc" and not (first and g == 0):
                                acc_tile(b0, g0, t)
                            elif kind == "ffn" and not first:
                                ffn_tile(b - 1, g, t)
                    take_y(b, g, 1)
                    if not first:
                        experts(b - 1, g)

            dve.sem_inc(taken["ffn"], 1)
            dve.sem_inc(taken["gen"], 1)
            nc.vector.memset(y_ps[:, :], 0.0)
            dve.wait_ge(loaded, 16 * LOADS)
            for k in range(KC):
                for g in range(G):
                    for a in range(2):
                        src = stage[:, k, a * D + g * HG * DH:a * D + (g + 1) * HG * DH].rearrange("p (h d) -> p d h", d=DH)
                        dst = [w_qk[:, k, g, w, a * HG * DH:(a + 1) * HG * DH].rearrange("p (d h) -> p d h", h=HG)
                               for w in range(2)]
                        nc.vector.tensor_copy(dst[0], src)
                        nc.vector.tensor_copy(dst[1][:, 0::2, :], src[:, 1::2, :])
                        last = nc.vector.tensor_copy(dst[1][:, 1::2, :], src[:, 0::2, :])
            last.then_inc(weights_ready, 1)
            settle()
            nc.vector.memset(gap[:, :], 0.0).then_inc(stage_free, 1)
            dve.wait_ge(x_loaded, 16)
            layernorm_stats(lambda i: x_in[:, i, :], NB, 0)
            for t in range(4):
                xt_tile(0, t, True)
            for t in range(4):
                qk_tile(0, 0, t, True)
            batch(0, True, False)
            with dve.Fori(1, B - 1) as b:
                batch(b, False, False)
            batch(B - 1, False, True)
            last_b = B - 1
            reciprocals(last_b, G - 1)
            for t in range(2):
                norm_tile(last_b, G - 1, t)
            for t in range(4):
                acc_tile(last_b, G - 1, t)
            for g in range(G):
                ffn_prepare(last_b, g)
                for t in range(FFN_TILES):
                    if t == 3:
                        route(last_b, g)
                    ffn_tile(last_b, g, t)
                experts(last_b, g)


_INS = ['L0_attn_x', 'L0_attn_Wqkv', 'L0_attn_Wout', 'L0_attn_bout', 'L0_ffn_Ws1', 'L0_ffn_Ws2', 'L0_ffn_W1',
        'L0_ffn_W2', 'L0_ffn_Wr']


def rope_tables():
    i = np.arange(DH // 2, dtype=np.float32)
    theta = np.power(np.float32(10000.0), np.float32(-2.0) * (i - np.float32(1.0)) / np.float32(DH))
    angle = np.arange(C, dtype=np.float32)[None, :] * theta[:, None]
    d = (np.arange(P) % (DH * HG)) // HG
    sign = np.where(d % 2 == 0, np.float32(-1.0), np.float32(1.0))
    cos, sin = np.cos(angle)[d // 2], np.sin(angle)[d // 2] * sign[:, None]
    return np.ascontiguousarray(cos, np.float32), np.ascontiguousarray(sin, np.float32)


def kernel(**inputs):
    import numpy as _np
    import concourse.bacc as _bacc
    from concourse import mybir as _mybir
    from concourse.bass_utils import run_bass_kernel_spmd as _run

    nc = _bacc.Bacc("TRN2", target_bir_lowering=False, num_devices=1)
    arrays, args = {}, []
    for name in _INS:
        a = _np.ascontiguousarray(inputs[name])
        arrays[f"in_{name}"] = a
        args.append(nc.dram_tensor(f"in_{name}", a.shape, _mybir.dt.from_np(a.dtype), kind="ExternalInput").ap())
    for name, a in zip(("cos", "sin"), rope_tables()):
        arrays[f"in_{name}"] = a
        args.append(nc.dram_tensor(f"in_{name}", a.shape, _mybir.dt.from_np(a.dtype), kind="ExternalInput").ap())
    args.append(nc.dram_tensor("out_0", (B, C, D), _mybir.dt.float32, kind="ExternalOutput").ap())
    block(nc, *args)
    r = _run(nc, [arrays], core_ids=[0])
    return r.results[0]["out_0"]
```

```python
import concourse.bass as bass
from concourse import mybir
from contextlib import ExitStack
import numpy as np


F32 = mybir.dt.float32
BF16 = mybir.dt.bfloat16
I32 = mybir.dt.int32
ALU = mybir.AluOpType
ACT = mybir.ActivationFunctionType
AXIS_X = mybir.AxisListType.X

B, C, D = 8, 1024, 256
H, DH = 16, 16
HG = 4
G = H // HG
P = 128
NB = C // P
KC = D // P
E, F = 8, 128
HALF = C // 2
PARTS, TERMS = 3, 6
ROWS = TERMS * DH
EPS = 1e-5
SCALE = 1.0 / DH ** 0.5
RING = 3


CHUNKS = [
    [(0, 0, 0, 512, 512), (1, 0, 1, 512, 512)],
    [(0, 0, 2, 512, 512), (1, 0, 3, 512, 512)],
    [(0, 0, 4, 512, 512), (1, 0, 7, 896, 128), (1, 128, 5, 640, 384)],
    [(0, 0, 0, 0, 512), (1, 0, 6, 768, 256), (1, 256, 2, 256, 256)],
    [(0, 0, 1, 128, 384), (0, 384, 3, 384, 128)],
]
DIAGONALS = {2: [(0, 2, 512), (640, 1, 0)], 3: [(0, 2, 512), (768, 1, 0)], 4: [(0, 2, 384)]}
MASKS = {c: len(d) * HG for c, d in DIAGONALS.items()}
MASKS_UNIT = sum(MASKS.values())


def unit_steps():
    steps, dens = [], [("den", j, i) for j in range(HG) for i in range(NB)]
    for c, count in zip(range(5), (7, 7, 6, 6, 6)):
        steps += [("num", c, j) for j in (range(HG) if c < 4 else range(0, HG, 2))]
        steps += [dens.pop(0) for _ in range(count)]
    return steps


STEPS = unit_steps()
NSTEP = len(STEPS)
LAST_STEP = {c: max(s for s, x in enumerate(STEPS) if x[:2] == ("num", c)) for c in range(5)}
FIRST_DEN = next(s for s, x in enumerate(STEPS) if x[0] == "den")

PV_AT = {8: (0, 0), 10: (0, 1), 18: (1, 0), 20: (1, 1), 30: (2, 0), 31: (2, 1), 32: (2, 2),
         40: (3, 1), 42: (3, 0), 43: (3, 2), 47: (4, 0), 49: (4, 1)}
PV_LAST = {10, 20, 32, 43, 49}
Y_FIRST, Y_LAST = {8: 0, 42: 1}, {40, 49}
TAKE_Y = 41

SIDE = [
    {0: ("v", 0), 2: ("v", 1), 4: ("v", 2), 6: ("v", 3),
     12: ("qk", 0), 19: ("qk", 1), 22: ("qk", 2), 28: ("qk", 3)},
    {0: ("qk", 0), 7: ("qk", 1), 11: ("qk", 2), 17: ("qk", 3), 22: ("norm", 0), 24: ("norm", 1),
     26: ("acc", 0), 28: ("acc", 1), 34: ("acc", 2), 36: ("acc", 3)},
    {0: ("qk", 0), 4: ("t2", 0), 7: ("qk", 1), 9: ("t2", 1), 11: ("qk", 2), 15: ("t2", 2), 17: ("qk", 3),
     19: ("t2", 3), 21: ("route", 0), 23: ("route", 1), 25: ("route", 2), 27: ("route", 3),
     29: ("norm", 0), 33: ("norm", 1), 35: ("route", 4), 36: ("acc", 0), 38: ("acc", 1), 41: ("acc", 2),
     44: ("acc", 3)},
    {0: ("xt", 0), 2: ("xt", 1), 4: ("xt", 2), 6: ("xt", 3), 11: ("qk", 0), 14: ("ffn", 0), 16: ("ffn", 1),
     19: ("qk", 1), 21: ("qk", 2), 24: ("ffn", 2), 27: ("qk", 3), 29: ("ffn", 3), 33: ("ffn", 4),
     35: ("ffn", 5), 37: ("ffn", 6), 39: ("ffn", 7)},
]
IN_TWO = {("v", 0), ("v", 1), ("v", 2), ("v", 3), ("qk", 0), ("qk", 2)}
PAIR_OF = {1: 1, 2: 0}
TILES = {"v": 4, "xt": 4, "qk": 4 * G, "norm": 4, "acc": 8, "t2": 4, "route": 5, "ffn": 8, "gen": 12 * E}
STATS2 = (1, 44)
STATS1 = (2, 33)
COPY = (1, 44)
GAP = (2, 28)
BRANCH = (2, 46)


def runs(kind, g, first, last):
    if first and (kind in ("t2", "route", "ffn") or kind in ("norm", "acc") and PAIR_OF[g] == 1):
        return False
    return not (last and (kind == "xt" or kind == "qk" and g == G - 1))


def block(nc, x, w_qkv, w_out, b_out, ws1, ws2, w1, w2, wr, cos_in, sin_in, out):
    x_v = x.rearrange("b (n p) d -> b p n d", p=P)
    out_v = out.rearrange("b (n p) d -> b p n d", p=P)
    scratch = nc.dram_tensor("qk_parts", (2, PARTS, 2, DH * HG, C), BF16, kind="Internal").ap()

    with ExitStack() as ctx:
        def sb(name, shape, dt=F32):
            return ctx.enter_context(nc.sbuf_tensor(name, shape, dt))

        def ps(name, shape):
            return ctx.enter_context(nc.psum_tensor(name, shape, F32))

        def sem(name):
            return ctx.enter_context(nc.semaphore(name))

        stack = sb("stack", [P, 2, 2, 2, HG * C], BF16)
        probs = sb("probs", [P, 2, HG, C])
        x_in = sb("x_in", [P, NB, D])
        xn = sb("xn", [P, 2, D])
        xnt = sb("xnt", [P, KC, C])
        v_sb = sb("v_sb", [P, NB, H, 2, DH])
        x_acc = sb("x_acc", [P, NB, D])
        x_mid = sb("x_mid", [P, NB, D])
        y_sb = sb("y_sb", [P, 2, C])
        w_qk = sb("w_qk", [P, KC, G, P])
        swap = sb("swap", [P, P], BF16)
        w_v = sb("w_v", [P, KC, D])
        w_o = sb("w_o", [P, 2, D])
        ws1_sb = sb("ws1_sb", [P, KC, F])
        ws2_sb = sb("ws2_sb", [P, D])
        wr_sb = sb("wr_sb", [P, KC, E])
        cos_sb = sb("cos_sb", [P, C])
        sin_sb = sb("sin_sb", [P, C])
        bias = sb("bias", [P, D])
        ident = sb("ident", [P, P])
        ones = sb("ones", [P, P])
        parts = sb("parts", [P, 2, PARTS, HALF], BF16)
        rest = sb("rest", [P, HALF])
        rot = sb("rot", [P, HALF])
        den = sb("den", [P, 2, NB, HG])
        rden = sb("rden", [P, NB, 2, HG])
        spread = [rest[:, :], rot[:, :]]
        stats = sb("stats", [P, NB, 6])
        mean_var = sb("mean_var", [P, 2, NB, 2])
        rstd = sb("rstd", [P, 2, NB])
        root = [sb(f"root{i}", [P, NB]) for i in range(3)]
        xn2t = sb("xn2t", [P, KC, C])
        hidden = sb("hidden", [P, 2 * P])
        hidden2 = sb("hidden2", [P, 2 * P])
        logits_t = sb("logits_t", [E, HALF])
        logits = sb("logits", [P, NB, E])
        top = sb("top", [P, NB, 8])
        gap = sb("gap", [P, NB])
        gap_exp = sb("gap_exp", [P, NB])
        weight = sb("weight", [P, NB])
        prob = sb("prob", [P, NB, E])
        routed = sb("routed", [1, 1])
        routed_i = sb("routed_i", [1, 1], I32)
        gate = sb("gate", [P, 2 * P])
        w1_now = sb("w1_now", [P, KC, F])
        w2_now = sb("w2_now", [P, D])
        y_out = sb("y_out", [P, 2, D])

        scores = ps("scores", [P, RING, 2 * HALF])
        y_ps = ps("y_ps", [P, HALF])
        side = ps("side", [P, HALF])

        loaded = sem("loaded")
        consts = sem("consts")
        weights_ready = sem("weights_ready")
        stage_free = sem("stage_free")
        x_loaded = sem("x_loaded")
        plain_sent = sem("plain_sent")
        rot_sent = sem("rot_sent")
        stacked = [sem("stacked0"), sem("stacked1")]
        out_sent = sem("out_sent")
        scores_ready = sem("scores_ready")
        exp_done = sem("exp_done")
        masked = sem("masked")
        chunk_used = sem("chunk_used")
        y_ready = sem("y_ready")
        y_taken = sem("y_taken")
        spread_ready = sem("spread_ready")
        den_used = sem("den_used")
        full = {k: sem(f"{k}_full") for k in TILES}
        taken = {k: sem(f"{k}_taken") for k in TILES}
        xn_ready = sem("xn_ready")
        xn2_ready = sem("xn2_ready")
        middle_ready = sem("middle_ready")
        low_ready = sem("low_ready")
        x_acc_used = sem("x_acc_used")
        x_copied = sem("x_copied")
        gap_ready = sem("gap_ready")
        gap_exped = sem("gap_exped")
        weight_ready = sem("weight_ready")
        hidden_ready = sem("hidden_ready")
        routed_ready = sem("routed_ready")
        expert_loaded = sem("expert_loaded")
        gate_ready = sem("gate_ready")
        y_out_ready = sem("y_out_ready")

        program = ctx.enter_context(nc.Block())
        LOADS = 16

        held = {e: sem(f"held_{e}") for e in ("sp", "pool", "pe", "dve")}

        def at1(b, per, k):
            return b * per + k + 1

        def score_tile(n):
            return scores[:, n % RING, :]

        def at(b, per, k):
            return b * per + k

        stage = probs[:, 0, 0, 0:KC * 2 * D].rearrange("p (k n) -> p k n", k=KC)

        @program.sync
        def _(sp):
            sp.dma_start(stage, w_qkv.rearrange("(k p) n -> p k n", p=P)[:, :, 0:2 * D]).then_inc(loaded, 16)
            sp.dma_start(x_in[:, :, :], x_v[0]).then_inc(x_loaded, 16)
            sp.dma_start(w_v[:, :, :], w_qkv.rearrange("(k p) n -> p k n", p=P)[:, :, 2 * D:3 * D]).then_inc(loaded, 16)
            sp.dma_start(cos_sb[:, :], cos_in).then_inc(loaded, 16)
            sp.dma_start(sin_sb[:, :], sin_in).then_inc(loaded, 16)
            wo_v = w_out.rearrange("(p a j d) n -> a j d p n", p=2, a=2, j=HG)
            for a in range(2):
                for j in range(HG):
                    sp.dma_start(w_o[32 * j + DH * a:32 * j + DH * (a + 1), :, :], wo_v[a, j]).then_inc(loaded, 16)
            sp.dma_start(bias[:, :], b_out.rearrange("(a n) -> a n", a=1).to_broadcast([P, D])).then_inc(loaded, 16)
            sp.dma_start(ws1_sb[:, :, :], ws1.rearrange("(k p) f -> p k f", p=P)).then_inc(loaded, 16)
            sp.dma_start(ws2_sb[:, :], ws2).then_inc(loaded, 16)
            sp.dma_start(wr_sb[:, :, :], wr.rearrange("(k p) e -> p k e", p=P)).then_inc(loaded, 16)

            def send_parts(b, g, outs=None):
                parity = g % 2
                if not (isinstance(b, int) and b == 0 and g == 0):
                    sp.wait_ge(stacked[1 - parity], at(b, 2 * 12 * 16, (g + parity) // 2 * 12 * 16))
                    sp.sem_inc(held["sp"], 1)
                for half in range(2):
                    for kind, sent in ((0, plain_sent), (1, rot_sent)):
                        sp.wait_ge(low_ready, at(b, 16, 4 * g + 2 * half + kind + 1))
                        sp.sem_inc(held["sp"], 1)
                        sp.dma_start(scratch[kind, :, :, :, half * HALF:(half + 1) * HALF].rearrange("c s r t -> (s r) c t"),
                                     parts[:, kind, :, :]).then_inc(sent, 16)
                    if outs is not None:
                        send_out(outs, half)
                if not (isinstance(b, int) and b == 0 and g < 2):
                    sp.wait_ge(scores_ready, at(b, G * NSTEP, (g - 1) * NSTEP))
                    sp.sem_inc(held["sp"], 1)
                for kind, sent in ((0, plain_sent), (1, rot_sent)):
                    sp.wait_ge(sent, at(b, 8 * 16, 2 * 16 * (g + 1)))
                    sp.sem_inc(held["sp"], 1)
                    src = scratch[kind].rearrange("c s (d h) t -> c s d (h t)", h=HG)
                    for side_no, runs in ((0, [(0, 1), (0, 1), (0, 1), (1, 1), (1, 1), (2, 1)]),
                                          (1, [(0, 3), (0, 2), (0, 1)])):
                        row = 0
                        if side_no == 0:
                            for part, copies in ((0, 3), (1, 2), (2, 1)):
                                s = src[part, 0]
                                if copies > 1:
                                    s = s.unsqueeze(0).to_broadcast([copies, DH, HG * C])
                                sp.dma_start(stack[row:row + copies * DH, parity, kind, 0, :], s).then_inc(stacked[parity], 16)
                                row += copies * DH
                        else:
                            for first, n in runs:
                                sp.dma_start(stack[row:row + n * DH, parity, kind, 1, :],
                                             src[0:n, 1]).then_inc(stacked[parity], 16)
                                row += n * DH

            def batch(b, first, last):
                for g in range(G):
                    if g < G - 1:
                        send_parts(b, g + 1)
                    elif not last:
                        send_parts(b + 1, 0, None if first else b - 1)
                    if g == 1 and not last:
                        sp.wait_ge(x_copied, at(b, 1, 1))
                        sp.sem_inc(held["sp"], 1)
                        sp.dma_start(x_in[:, :, :], x_v[b + 1]).then_inc(x_loaded, 16)
                if not first:
                    for pair in range(0 if last else 2, G):
                        send_out(b - 1, pair)

            def send_out(b, g):
                sp.wait_ge(y_out_ready, at(b, G, g + 1))
                sp.sem_inc(held["sp"], 1)
                sp.dma_start(out_v[b][:, 2 * g:2 * g + 2, :], y_out[:, :, :]).then_inc(out_sent, 16)

            sp.sem_inc(out_sent, 1)
            send_parts(0, 0)
            batch(0, True, False)
            with sp.Fori(1, B - 1) as b:
                batch(b, False, False)
            batch(B - 1, False, True)
            for g in range(G):
                send_out(B - 1, g)
            sp.wait_ge(out_sent, at1(B, 16 * G, 0))

        @program.gpsimd
        def _(pool):
            nc.gpsimd.memset(ones[:, :], 1.0).then_inc(consts, 1)
            nc.gpsimd.memset(ident[:, :], 0.0).then_inc(consts, 1)
            nc.gpsimd.memset(swap[:, :], 0.0).then_inc(consts, 1)
            nc.gpsimd.memset(v_sb[:, :, :, :, :], 0.0).then_inc(consts, 1)
            pool.wait_ge(consts, 4)
            swap_v = swap[:, :].rearrange("p (u w v) -> p w u v", w=2, v=HG)
            for w in range(2):
                nc.gpsimd.affine_select(out=swap_v[:, w], in_=swap_v[:, w], compare_op=ALU.not_equal, fill=1.0,
                                        base=-HG * (1 - w), pattern=[[-2 * HG, P // (2 * HG)], [-1, HG]],
                                        channel_multiplier=1).then_inc(consts, 1)
            nc.gpsimd.affine_select(out=ident[:, :], in_=ident[:, :], compare_op=ALU.not_equal, fill=1.0, base=0,
                                    pattern=[[-1, P]], channel_multiplier=1).then_inc(consts, 1)

            def mask(b, g, c):
                for j in range(HG):
                    step = LAST_STEP[c] - (HG - 1 - j if c < 4 else 1 - j // 2)
                    pool.wait_ge(exp_done, at(b, G * NSTEP, g * NSTEP + step + 1))
                    pool.sem_inc(held["pool"], 1)
                    for col, n, stride in DIAGONALS[c]:
                        p = probs[:, (5 * g + c) % 2, j, :]
                        if n == 1:
                            v, pattern = p[:, col:col + P], [[1, P]]
                        else:
                            v = p[:, col:col + n * stride].rearrange("p (n s) -> p n s", n=n)[:, :, 0:P]
                            pattern = [[0, n], [1, P]]
                        nc.gpsimd.affine_select(out=v, in_=v, compare_op=ALU.is_ge, fill=0.0, base=0,
                                                pattern=pattern, channel_multiplier=-1).then_inc(masked, 1)

            def low_part(b, g, t):
                pool.wait_ge(middle_ready, at(b, 16, 4 * g + t + 1))
                nc.gpsimd.tensor_tensor(parts[:, t % 2, 2, :], rest[:, :], parts[:, t % 2, 1, :], ALU.subtract
                                        ).then_inc(low_ready, 1)

            def load_experts(b):
                pool.wait_ge(routed_ready, at(b, 1, 1))
                pool.sem_inc(held["pool"], 1)
                count = pool.value_load(routed_i[0:1, 0:1], min_val=0, max_val=C)
                with pool.If(count > 0):
                    with pool.Fori(0, E) as e:
                        pool.wait_ge(taken["gen"], at1(b, TILES["gen"], 0) + e * 12)
                        pool.sem_inc(held["pool"], 1)
                        pool.dma_start(w1_now[:, :, :], w1[bass.ds(e, 1)].rearrange("e (k p) f -> p (e k) f", p=P)
                                       ).then_inc(expert_loaded, 16)
                        pool.dma_start(w2_now[:, :], w2[bass.ds(e, 1)].rearrange("e f d -> f (e d)")
                                       ).then_inc(expert_loaded, 16)
                with pool.Else():
                    pool.sem_inc(expert_loaded, 32 * E)

            def batch(b, first, last):
                for g in range(G):
                    for s in range(NSTEP):
                        if (g, s) == COPY:
                            if not first:
                                pool.wait_ge(x_acc_used, at(b, 1, 0))
                            else:
                                pool.wait_ge(x_loaded, 16)
                            nc.gpsimd.tensor_tensor(x_acc[:, :, :], x_in[:, :, :],
                                                    bias[:, :].unsqueeze(1).to_broadcast([P, NB, D]), ALU.add
                                                    ).then_inc(x_copied, 1)
                        if s in SIDE[g] and SIDE[g][s][0] == "qk" and runs("qk", g, first, last):
                            b1, g1 = (b, g + 1) if g < G - 1 else (b + 1, 0)
                            low_part(b1, g1, SIDE[g][s][1])
                        for c in DIAGONALS:
                            if s == LAST_STEP[c] + 1:
                                mask(b, g, c)
                        if (g, s) == BRANCH and not first:
                            load_experts(b - 1)

            pool.wait_ge(loaded, 16 * LOADS)
            for t in range(4):
                low_part(0, 0, t)
            batch(0, True, False)
            with pool.Fori(1, B - 1) as b:
                batch(b, False, False)
            batch(B - 1, False, True)
            load_experts(B - 1)

        @program.scalar
        def _(act):
            def batch(b, first):
                for g in range(G):
                    for s, step in enumerate(STEPS):
                        act_step(b, first, g, s, step)
                        if (g, s) == GAP and not first:
                            exp_gap(b - 1)

            def act_step(b, first, g, s, step):
                n = g * NSTEP + s
                act.wait_ge(scores_ready, at(b, G * NSTEP, n + 1))
                src = score_tile(n)
                if step[0] == "den":
                    _, j, i = step
                    if s == FIRST_DEN and not (first and g < 2):
                        act.wait_ge(den_used, at(b, G, g - 1))
                    nc.scalar.activation(src, src, ACT.Exp, scale=SCALE,
                                         accum_out=den[:, g % 2, i, j:j + 1]).then_inc(exp_done, 1)
                    return
                _, c, j = step
                chunk = 5 * g + c
                if j == 0 and not (first and chunk < 2):
                    act.wait_ge(chunk_used, at(b, 5 * G, chunk - 1))
                if j == 0 and first and chunk < 2:
                    act.wait_ge(stage_free, 1)
                if c < 4:
                    nc.scalar.activation(probs[:, chunk % 2, j, :], src, ACT.Exp, scale=SCALE).then_inc(exp_done, 1)
                else:
                    nc.scalar.activation(probs[:, chunk % 2, j:j + 2, 0:HALF], src.rearrange("p (a n) -> p a n", a=2),
                                         ACT.Exp, scale=SCALE).then_inc(exp_done, 1)

            def exp_gap(b):
                act.wait_ge(gap_ready, at(b, 1, 1))
                nc.scalar.activation(gap_exp[:, :], gap[:, :], ACT.Exp).then_inc(gap_exped, 1)

            batch(0, True)
            with act.Fori(1, B) as b:
                batch(b, False)
            exp_gap(B - 1)

        @program.tensor
        def _(pe):
            pe.wait_ge(loaded, 16 * LOADS)
            pe.wait_ge(consts, 7)

            def scores_step(b, first, g, s, step):
                n = g * NSTEP + s
                if n >= RING:
                    pe.wait_ge(exp_done, at(b, G * NSTEP, n - RING + 1))
                elif not first:
                    user = max(m for m in range(G * NSTEP) if m % RING == n)
                    pe.wait_ge(exp_done, at(b - 1, G * NSTEP, user + 1))
                tile = score_tile(n)
                q, k = (stack[0:ROWS, g % 2, 0 if step[0] == "den" else 1, a, :].rearrange("p (h t) -> p h t", h=HG)
                        for a in (0, 1))
                if step[0] == "den":
                    _, j, i = step
                    for half in range(2):
                        mm = nc.tensor.matmul(tile[:, half * HALF:(half + 1) * HALF], q[:, j, i * P:(i + 1) * P],
                                              k[:, j, half * HALF:(half + 1) * HALF], start=True, stop=True)
                else:
                    _, c, j = step
                    for h in ((j,) if c < 4 else (j, j + 1)):
                        for bank, col, i, q0, n in CHUNKS[c]:
                            col += (bank + h - j) * HALF
                            mm = nc.tensor.matmul(tile[:, col:col + n], k[:, h, i * P:(i + 1) * P], q[:, h, q0:q0 + n],
                                                  start=True, stop=True)
                mm.then_inc(scores_ready, 1)

            def heads_step(b, first, g, s):
                c, piece = PV_AT[s]
                bank, col, i, q0, n = CHUNKS[c][piece]
                col += bank * HALF
                if s in Y_FIRST and not (first and g == 0 and Y_FIRST[s] == 0):
                    pe.wait_ge(y_taken, at(b, 2 * G, 2 * g + Y_FIRST[s]))
                if g == 0:
                    pe.wait_ge(taken["v"], at(b, 4, i // 2 + 1))
                if c in MASKS:
                    done = sum(m for k, m in MASKS.items() if k <= c)
                    pe.wait_ge(masked, at(b, G * MASKS_UNIT, g * MASKS_UNIT + done))
                else:
                    pe.wait_ge(exp_done, at(b, G * NSTEP, g * NSTEP + LAST_STEP[c] + 1))
                o0 = q0 % HALF
                for j in range(HG):
                    h = g * HG + j
                    mm = nc.tensor.matmul(y_ps[32 * j:32 * j + 32, o0:o0 + n], v_sb[:, i, h, :, :],
                                          probs[:, (5 * g + c) % 2, j, col:col + n], start=s in Y_FIRST, stop=s in Y_LAST,
                                          tile_position=(0, 32 * j), skip_group_check=True)
                if s in PV_LAST:
                    mm.then_inc(chunk_used, 1)
                elif s in Y_LAST:
                    mm.then_inc(y_ready, 1)

            def v_tile(b, t, i):
                for k in range(KC):
                    mm = nc.tensor.matmul(side[:, i * D:(i + 1) * D], xnt[:, k, (2 * t + i) * P:(2 * t + i + 1) * P],
                                          w_v[:, k, :], start=k == 0, stop=k == KC - 1)
                if i == 1:
                    mm.then_inc(full["v"], 1)

            def xt_tile(b, t):
                pe.wait_ge(xn_ready, at(b, 4, t + 1))
                for k in range(KC):
                    for i in range(2):
                        mm = nc.tensor.transpose(side[:, (2 * k + i) * P:(2 * k + i + 1) * P], xn[:, i, k * P:(k + 1) * P],
                                                 ident[:, :])
                mm.then_inc(full["xt"], 1)

            def qk_tile(b, g, t, k):
                half = t // 2
                if t % 2 == 0:
                    if t == 0 and k == 0 and g == 0:
                        pe.wait_ge(taken["xt"], at(b, 4, 4))
                    mm = nc.tensor.matmul(side[:, :], w_qk[:, k, g, :], xnt[:, k, half * HALF:(half + 1) * HALF],
                                          start=k == 0, stop=k == KC - 1)
                    if k == 0:
                        return
                else:
                    pe.wait_ge(low_ready, at(b, 16, 4 * g + t))
                    for i in range(PARTS):
                        mm = nc.tensor.matmul(side[:, :], swap[:, :], parts[:, 0, i, :], start=i == 0, stop=i == PARTS - 1)
                mm.then_inc(full["qk"], 1)

            def norm_tile(b, pair, t):
                pe.wait_ge(spread_ready, at(b, 4, 2 * pair + t + 1))
                for i in range(NB // 2):
                    mm = nc.tensor.transpose(side[:, i * P:(i + 1) * P], spread[t][:, i * P:(i + 1) * P], ident[:, :])
                mm.then_inc(full["norm"], 1)

            def acc_tile(b, pair, t):
                if t == 0:
                    pe.wait_ge(taken["norm"], at(b, 4, 2 * pair + 2))
                for i in range(2):
                    mm = nc.tensor.matmul(side[:, i * D:(i + 1) * D], y_sb[:, pair, (2 * t + i) * P:(2 * t + i + 1) * P],
                                          w_o[:, pair, :], start=True, stop=True)
                mm.then_inc(full["acc"], 1)

            def t2_tile(b, t):
                pe.wait_ge(xn2_ready, at(b, 4, t + 1))
                for k in range(KC):
                    for i in range(2):
                        mm = nc.tensor.transpose(side[:, (2 * k + i) * P:(2 * k + i + 1) * P], xn[:, i, k * P:(k + 1) * P],
                                                 ident[:, :])
                mm.then_inc(full["t2"], 1)

            def route_tile(b, t):
                if t < 4 and t % 2 == 0:
                    cols = slice(t // 2 * HALF, (t // 2 + 1) * HALF)
                    pe.wait_ge(taken["t2"], at(b, 4, t + 2))
                    for k in range(KC):
                        mm = nc.tensor.matmul(side[0:E, :], wr_sb[:, k, :], xn2t[:, k, cols], start=k == 0, stop=k == KC - 1)
                elif t < 4:
                    pe.sem_inc(held["pe"], 1)
                    for i in range(NB // 2):
                        mm = nc.tensor.transpose(side[:, i * E:(i + 1) * E], logits_t[:, i * P:(i + 1) * P], ident[0:E, 0:E])
                else:
                    pe.wait_ge(weight_ready, at(b, 1, 1))
                    mm = nc.tensor.matmul(side[:, 0:NB], ones[:, :], weight[:, :], start=True, stop=True)
                mm.then_inc(full["route"], 1)

            def ffn_tile(b, t):
                pair = t // 2
                if t % 2 == 0:
                    for k in range(KC):
                        mm = nc.tensor.matmul(side[:, 0:2 * P], ws1_sb[:, k, :], xn2t[:, k, 2 * pair * P:2 * (pair + 1) * P],
                                              start=k == 0, stop=k == KC - 1)
                else:
                    pe.wait_ge(hidden_ready, at(b, 4, pair + 1))
                    for i in range(2):
                        mm = nc.tensor.matmul(side[:, i * D:(i + 1) * D], hidden2[:, i * P:(i + 1) * P], ws2_sb[:, :],
                                              start=True, stop=True)
                mm.then_inc(full["ffn"], 1)

            def experts(b):
                pe.wait_ge(routed_ready, at(b, 1, 1))
                pe.sem_inc(held["pe"], 1)
                count = pe.value_load(routed_i[0:1, 0:1], min_val=0, max_val=C)
                with pe.If(count > 0):
                    with pe.Fori(0, E) as e:
                        base = at1(b, TILES["gen"], 0) + e * 12
                        pe.wait_ge(expert_loaded, at(b, 32 * E, 32) + e * 32)
                        pe.sem_inc(held["pe"], 1)
                        for pair in range(4):
                            pe.wait_ge(gate_ready, at(b, 4 * E, pair + 1) + e * 4)
                            pe.wait_ge(taken["gen"], base + 3 * pair)
                            for i in range(2):
                                mm = nc.tensor.transpose(side[:, i * P:(i + 1) * P], gate[:, i * P:(i + 1) * P], ident[:, :])
                            mm.then_inc(full["gen"], 1)
                            pe.wait_ge(taken["gen"], base + (3 * pair + 1))
                            for k in range(KC):
                                mm = nc.tensor.matmul(side[:, 0:2 * P], w1_now[:, k, :], xn2t[:, k, 2 * pair * P:2 * (pair + 1) * P],
                                                      start=k == 0, stop=k == KC - 1)
                            mm.then_inc(full["gen"], 1)
                            pe.wait_ge(taken["gen"], base + (3 * pair + 2))
                            for i in range(2):
                                mm = nc.tensor.matmul(side[:, i * D:(i + 1) * D], hidden[:, i * P:(i + 1) * P], w2_now[:, :],
                                                      start=True, stop=True)
                            mm.then_inc(full["gen"], 1)
                with pe.Else():
                    pe.sem_inc(full["gen"], TILES["gen"])

            def tile_of(b, g, kind, t):
                if kind == "qk":
                    return (b, 4 * (g + 1) + t) if g < G - 1 else (b + 1, t)
                if kind in ("norm", "acc"):
                    pair = PAIR_OF[g]
                    return b - pair, TILES[kind] // 2 * pair + t
                return (b if kind == "v" else b + 1 if kind == "xt" else b - 1), t

            def side_step(b, first, last, g, s, before):
                second = (s - 1) in SIDE[g] and SIDE[g][s - 1] in IN_TWO
                if not second and s not in SIDE[g]:
                    return before
                kind, t = SIDE[g][s - 1 if second else s]
                if not runs(kind, g, first, last):
                    return before
                bb, n = tile_of(b, g, kind, t)
                if not second:
                    for k0, b0, n0 in before:
                        pe.wait_ge(taken[k0], (at1 if k0 in ("ffn", "gen") else at)(b0, TILES[k0], n0 + 1))
                if kind == "v":
                    v_tile(bb, t, int(second))
                elif kind == "xt":
                    xt_tile(bb, t)
                elif kind == "qk":
                    qk_tile(bb, n // 4, t, int(second))
                elif kind == "norm":
                    norm_tile(bb, n // 2, t)
                elif kind == "acc":
                    acc_tile(bb, n // 4, t)
                elif kind == "t2":
                    t2_tile(bb, t)
                elif kind == "route":
                    route_tile(bb, t)
                else:
                    ffn_tile(bb, t)
                return [(kind, bb, n)]

            def batch(b, first, last):
                before = [("qk", b, 3)] + ([] if first else [("ffn", b - 2, TILES["ffn"] - 1)])
                for g in range(G):
                    parity = g % 2
                    pe.wait_ge(stacked[parity], at(b, 2 * 12 * 16, (g // 2 + 1) * 12 * 16))
                    for s, step in enumerate(STEPS):
                        scores_step(b, first, g, s, step)
                        if s in PV_AT:
                            heads_step(b, first, g, s)
                        before = side_step(b, first, last, g, s, before)
                        if (g, s) == BRANCH and not first:
                            for k0, b0, n0 in before:
                                pe.wait_ge(taken[k0], at(b0, TILES[k0], n0 + 1))
                            experts(b - 1)
                            before = before + [("gen", b - 1, TILES["gen"] - 1)]

            pe.wait_ge(weights_ready, 1)
            for t in range(4):
                if t:
                    pe.wait_ge(taken["xt"], t)
                xt_tile(0, t)
            pe.wait_ge(taken["xt"], 4)
            for t in range(4):
                if t:
                    pe.wait_ge(taken["qk"], t)
                for k in range(KC if t % 2 == 0 else 1):
                    qk_tile(0, 0, t, k)
            batch(0, True, False)
            with pe.Fori(1, B - 1) as b:
                batch(b, False, False)
            batch(B - 1, False, True)
            last = B - 1
            pe.wait_ge(taken["ffn"], at1(last - 1, TILES["ffn"], TILES["ffn"]))
            for t in range(2):
                if t:
                    pe.wait_ge(taken["norm"], at(last, 4, 3))
                norm_tile(last, 1, t)
            for t in range(4):
                if t:
                    pe.wait_ge(taken["acc"], at(last, 8, 4 + t))
                acc_tile(last, 1, t)
            pe.wait_ge(taken["acc"], at(last, 8, 8))
            for t in range(4):
                if t:
                    pe.wait_ge(taken["t2"], at(last, 4, t))
                t2_tile(last, t)
            pe.wait_ge(taken["t2"], at(last, 4, 4))
            for t in range(TILES["route"]):
                if t:
                    pe.wait_ge(taken["route"], at(last, TILES["route"], t))
                route_tile(last, t)
            pe.wait_ge(taken["route"], at(last, TILES["route"], TILES["route"]))
            experts(last)
            pe.wait_ge(taken["gen"], at1(last, TILES["gen"], TILES["gen"]))
            for t in range(TILES["ffn"]):
                if t:
                    pe.wait_ge(taken["ffn"], at1(last, TILES["ffn"], t))
                ffn_tile(last, t)

        @program.vector
        def _(dve):
            def settle():
                dve.drain()

            def inverse_root(n, var, result):
                v, a, y = (r[:, 0:n] for r in root)
                nc.vector.tensor_scalar(v, var, EPS, None, ALU.add)
                settle()
                nc.vector.tensor_scalar(a.bitcast(I32), v.bitcast(I32), 1, None, ALU.logical_shift_right)
                settle()
                nc.vector.tensor_scalar(y.bitcast(I32), a.bitcast(I32), -1.0, float(0x5f3759df), ALU.mult, ALU.add)
                settle()
                for i in range(3):
                    nc.vector.scalar_tensor_tensor(a, y, -0.5, y, ALU.mult, ALU.mult)
                    settle()
                    nc.vector.tensor_tensor(a, a, v, ALU.mult)
                    settle()
                    nc.vector.scalar_tensor_tensor(result if i == 2 else y, a, 1.5, y, ALU.add, ALU.mult)
                    settle()

            def layernorm_stats(src, which):
                for i in range(NB):
                    nc.vector.bn_stats(stats[:, i, :], src[:, i, :])
                settle()
                for i in range(NB):
                    nc.vector.bn_aggr(mean_var[:, which, i, :], stats[:, i, :])
                settle()
                inverse_root(NB, mean_var[:, which, :, 1], rstd[:, which, :])

            def layernorm(src, which, t, ready):
                for i in range(2):
                    blk = 2 * t + i
                    last = nc.vector.tensor_scalar(xn[:, i, :], src[:, blk, :], mean_var[:, which, blk, 0:1],
                                                   rstd[:, which, blk:blk + 1], ALU.subtract, ALU.mult)
                last.then_inc(ready, 1)

            def v_tile(b, first, t):
                if t == 0 and not first:
                    dve.wait_ge(chunk_used, at(b, 5 * G, 0))
                dve.wait_ge(full["v"], at(b, 4, t + 1))
                for a in range(2):
                    src = side[:, :].rearrange("p (i q a c) -> p i q a c", i=2, a=2, c=HG * DH)[:, :, :, a, :]
                    for i in range(2):
                        last = nc.vector.tensor_copy(
                            v_sb[:, 2 * t + i, :, a, :].rearrange("p (q a h) d -> p q a h d", a=2, h=HG)[:, :, a],
                            src[:, i].rearrange("p q (h d) -> p q h d", d=DH))
                last.then_inc(taken["v"], 1)

            def xt_tile(b, t):
                dve.wait_ge(full["xt"], at(b, 4, t + 1))
                nc.vector.tensor_copy(xnt[:, :, 2 * t * P:(2 * t + 2) * P], side[:, :].rearrange("p (k n) -> p k n", k=KC)
                                      ).then_inc(taken["xt"], 1)
                if t < 3:
                    layernorm(x_in, 0, t + 1, xn_ready)

            def split(kind, src, low_before):
                nc.vector.tensor_copy(parts[:, kind, 0, :], src)
                settle()
                if low_before is not None:
                    dve.wait_ge(low_ready, low_before)
                nc.vector.tensor_tensor(rest[:, :], src, parts[:, kind, 0, :], ALU.subtract)

            def middle(kind):
                settle()
                nc.vector.tensor_copy(parts[:, kind, 1, :], rest[:, :]).then_inc(middle_ready, 1)

            def qk_tile(b, g, t, very_first):
                half = t // 2
                cols = slice(half * HALF, (half + 1) * HALF)
                dve.wait_ge(full["qk"], at(b, 16, 4 * g + t + 1))
                if not (very_first and half == 0):
                    dve.wait_ge((plain_sent, rot_sent)[t % 2], at(b, 8 * 16, 16 * (2 * g + half)))
                if t % 2 == 0:
                    split(0, side[:, :], None if very_first and t == 0 else at(b, 16, 4 * g + t))
                    nc.vector.tensor_tensor(rot[:, :], side[:, :], cos_sb[:, cols], ALU.mult).then_inc(taken["qk"], 1)
                    middle(0)
                else:
                    dve.wait_ge(low_ready, at(b, 16, 4 * g + t))
                    nc.vector.tensor_tensor(rest[:, :], side[:, :], sin_sb[:, cols], ALU.mult).then_inc(taken["qk"], 1)
                    settle()
                    nc.vector.tensor_tensor(rot[:, :], rot[:, :], rest[:, :], ALU.add)
                    settle()
                    split(1, rot[:, :], None)
                    middle(1)

            def reciprocals(b, g):
                dve.wait_ge(exp_done, at(b, G * NSTEP, (g + 1) * NSTEP))
                nc.vector.reciprocal(rden[:, :, g % 2, :], den[:, g % 2, :, :]).then_inc(den_used, 1)
                settle()

            def spread_reciprocals(lows):
                dve.wait_ge(low_ready, lows)
                for t in range(2):
                    blocks = slice((1 - t) * NB // 2, (2 - t) * NB // 2)
                    for a in range(2):
                        last = nc.vector.tensor_copy(
                            spread[t].rearrange("p (i h a r) -> p i h a r", h=HG, a=2, r=DH)[:, :, :, a, :],
                            rden[:, blocks, a, :].unsqueeze(3).to_broadcast([P, NB // 2, HG, DH]))
                    last.then_inc(spread_ready, 1)

            def take_y(b, g, t):
                if t == 0:
                    dve.wait_ge(y_ready, at(b, G, g + 1))
                else:
                    dve.wait_ge(chunk_used, at(b, 5 * G, 5 * (g + 1)))
                y = y_sb[:, g // 2, (1 - t) * HALF:(2 - t) * HALF]
                if g % 2 == 0:
                    nc.vector.tensor_copy(y, y_ps[:, :]).then_inc(y_taken, 1)
                else:
                    nc.vector.tensor_tensor(y, y_ps[:, :], y, ALU.add).then_inc(y_taken, 1)
                settle()

            def norm_tile(b, pair, t):
                dve.wait_ge(full["norm"], at(b, 4, 2 * pair + t + 1))
                y = y_sb[:, pair, (1 - t) * HALF:(2 - t) * HALF]
                nc.vector.tensor_tensor(y, side[:, :], y, ALU.mult).then_inc(taken["norm"], 1)

            def acc_tile(b, pair, t):
                if pair == 0 and t == 0:
                    dve.wait_ge(x_copied, at(b, 1, 1))
                blocks = slice(2 * t, 2 * t + 2)
                dve.wait_ge(full["acc"], at(b, 8, 4 * pair + t + 1))
                src = side[:, :].rearrange("p (i d) -> p i d", i=2)
                into = x_mid if pair else x_acc
                nc.vector.tensor_tensor(into[:, blocks, :], src, x_acc[:, blocks, :], ALU.add).then_inc(taken["acc"], 1)
                if pair and t == 3:
                    dve.drain().then_inc(x_acc_used, 1)

            def t2_tile(b, t):
                dve.wait_ge(full["t2"], at(b, 4, t + 1))
                nc.vector.tensor_copy(xn2t[:, :, 2 * t * P:(2 * t + 2) * P], side[:, :].rearrange("p (k n) -> p k n", k=KC)
                                      ).then_inc(taken["t2"], 1)
                if t < 3:
                    layernorm(x_mid, 1, t + 1, xn2_ready)

            def route_tile(b, t):
                dve.wait_ge(full["route"], at(b, TILES["route"], t + 1))
                if t in (0, 2):
                    nc.vector.tensor_copy(logits_t[:, :], side[0:E, :]).then_inc(taken["route"], 1)
                elif t in (1, 3):
                    blocks = slice(t // 2 * NB // 2, (t // 2 + 1) * NB // 2)
                    nc.vector.tensor_copy(logits[:, blocks, :], side[:, 0:NB // 2 * E].rearrange("p (i e) -> p i e", e=E)
                                          ).then_inc(taken["route"], 1)
                else:
                    nc.vector.tensor_reduce(routed[:, :], side[0:1, 0:NB], AXIS_X, ALU.add).then_inc(taken["route"], 1)
                    settle()
                    nc.vector.tensor_copy(routed_i[:, :], routed[:, :]).then_inc(routed_ready, 1)
                if t == 3:
                    settle()
                    for i in range(NB):
                        nc.vector.max(top[:, i, :], logits[:, i, :])
                    settle()
                    nc.vector.tensor_tensor(gap[:, :], top[:, :, 1], top[:, :, 0], ALU.subtract).then_inc(gap_ready, 1)

            def route(b):
                dve.wait_ge(gap_exped, at(b, 1, 1))
                nc.vector.tensor_scalar(weight[:, :], gap_exp[:, :], 1.0, None, ALU.add)
                settle()
                nc.vector.reciprocal(weight[:, :], weight[:, :])
                settle()
                nc.vector.tensor_scalar(weight[:, :], weight[:, :], 1.0, None, ALU.is_ge).then_inc(weight_ready, 1)

            def ffn_tile(b, t):
                pair = t // 2
                dve.wait_ge(full["ffn"], at(b, TILES["ffn"], t + 1))
                if t % 2 == 0:
                    nc.vector.tensor_scalar(hidden[:, :], side[:, 0:2 * P], 0.0, None, ALU.max).then_inc(taken["ffn"], 1)
                    settle()
                    nc.vector.tensor_tensor(hidden2[:, :], hidden[:, :], hidden[:, :], ALU.mult).then_inc(hidden_ready, 1)
                else:
                    dve.wait_ge(out_sent, at1(b, 16 * G, 16 * pair))
                    nc.vector.tensor_tensor(y_out[:, :, :], side[:, :].rearrange("p (i d) -> p i d", i=2),
                                            x_mid[:, 2 * pair:2 * pair + 2, :], ALU.add).then_inc(taken["ffn"], 1)
                    dve.drain().then_inc(y_out_ready, 1)

            def experts(b):
                dve.wait_ge(routed_ready, at(b, 1, 1))
                dve.sem_inc(held["dve"], 1)
                count = dve.value_load(routed_i[0:1, 0:1], min_val=0, max_val=C)
                with dve.If(count > 0):
                    for i in range(NB):
                        nc.vector.tensor_scalar(prob[:, i, :], logits[:, i, :], top[:, i, 0:1], weight[:, i:i + 1],
                                                ALU.is_equal, ALU.mult)
                    settle()
                    with dve.Fori(0, E) as e:
                        base = at(b, TILES["gen"], 0) + e * 12
                        for pair in range(4):
                            for i in range(2):
                                last = nc.vector.tensor_copy(gate[:, i * P:(i + 1) * P],
                                                             prob[:, 2 * pair + i, bass.ds(e, 1)].to_broadcast([P, P]))
                            last.then_inc(gate_ready, 1)
                            settle()
                            dve.wait_ge(full["gen"], base + (3 * pair + 1))
                            nc.vector.tensor_copy(gate[:, :], side[:, 0:2 * P]).then_inc(taken["gen"], 1)
                            settle()
                            dve.wait_ge(full["gen"], base + (3 * pair + 2))
                            nc.vector.scalar_tensor_tensor(hidden2[:, :], side[:, 0:2 * P], 0.0, gate[:, :], ALU.max, ALU.mult)
                            settle()
                            nc.vector.tensor_tensor(hidden[:, :], hidden2[:, :], hidden2[:, :], ALU.mult
                                                    ).then_inc(taken["gen"], 1)
                            dve.wait_ge(full["gen"], base + (3 * pair + 3))
                            x = x_mid[:, 2 * pair:2 * pair + 2, :]
                            nc.vector.tensor_tensor(x, side[:, :].rearrange("p (i d) -> p i d", i=2), x, ALU.add
                                                    ).then_inc(taken["gen"], 1)
                            settle()
                with dve.Else():
                    dve.sem_inc(taken["gen"], TILES["gen"])
                    dve.sem_inc(gate_ready, 4 * E)
                settle()

            def batch(b, first, last):
                for g in range(G):
                    b0, g0 = (b, g - 1) if g else (b - 1, G - 1)
                    for s in range(NSTEP):
                        kind, t = SIDE[g].get(s, ("none", 0))
                        if not runs(kind, g, first, last):
                            kind = "none"
                        if kind == "norm" and t == 0:
                            if g == 2:
                                reciprocals(b0, g0)
                            spread_reciprocals(at(b, 16, 12 if g == 1 else 16))
                        if s == 25 and g != 2 and not (first and g == 0):
                            reciprocals(b0, g0)
                        if (g, s) == STATS2 and not first:
                            layernorm_stats(x_mid, 1)
                            layernorm(x_mid, 1, 0, xn2_ready)
                        if (g, s) == STATS1 and not last:
                            dve.wait_ge(x_loaded, at(b, 16, 32))
                            layernorm_stats(x_in, 0)
                        if g == 3 and s == 0 and not last:
                            layernorm(x_in, 0, 0, xn_ready)
                        if s == TAKE_Y:
                            take_y(b, g, 0)
                        if kind == "v":
                            v_tile(b, first, t)
                        elif kind == "xt":
                            xt_tile(b + 1, t)
                        elif kind == "qk":
                            b1, g1 = (b, g + 1) if g < G - 1 else (b + 1, 0)
                            qk_tile(b1, g1, t, False)
                        elif kind == "norm":
                            norm_tile(b - PAIR_OF[g], PAIR_OF[g], t)
                        elif kind == "acc":
                            acc_tile(b - PAIR_OF[g], PAIR_OF[g], t)
                        elif kind == "t2":
                            t2_tile(b - 1, t)
                        elif kind == "route":
                            if t == 4:
                                route(b - 1)
                            route_tile(b - 1, t)
                        elif kind == "ffn":
                            ffn_tile(b - 1, t)
                        if (g, s) == BRANCH and not first:
                            experts(b - 1)
                    take_y(b, g, 1)

            dve.sem_inc(taken["ffn"], 1)
            dve.sem_inc(taken["gen"], 1)
            dve.wait_ge(loaded, 16 * LOADS)
            for k in range(KC):
                for g in range(G):
                    for a in range(2):
                        src = stage[:, k, a * D + g * HG * DH:a * D + (g + 1) * HG * DH].rearrange("p (h d) -> p d h", d=DH)
                        dst = w_qk[:, k, g, a * HG * DH:(a + 1) * HG * DH].rearrange("p (d h) -> p d h", h=HG)
                        last = nc.vector.tensor_copy(dst, src)
            last.then_inc(weights_ready, 1)
            dve.wait_ge(weights_ready, 1)
            nc.vector.memset(gap[:, :], 0.0).then_inc(stage_free, 1)
            dve.wait_ge(consts, 7)
            dve.wait_ge(x_loaded, 16)
            layernorm_stats(x_in, 0)
            layernorm(x_in, 0, 0, xn_ready)
            for t in range(4):
                xt_tile(0, t)
            for t in range(4):
                qk_tile(0, 0, t, True)
            batch(0, True, False)
            with dve.Fori(1, B - 1) as b:
                batch(b, False, False)
            batch(B - 1, False, True)
            last_b = B - 1
            reciprocals(last_b, G - 1)
            spread_reciprocals(at(last_b, 16, 16))
            for t in range(2):
                norm_tile(last_b, 1, t)
            for t in range(4):
                acc_tile(last_b, 1, t)
            layernorm_stats(x_mid, 1)
            layernorm(x_mid, 1, 0, xn2_ready)
            for t in range(4):
                t2_tile(last_b, t)
            for t in range(TILES["route"]):
                if t == 4:
                    route(last_b)
                route_tile(last_b, t)
            experts(last_b)
            for t in range(TILES["ffn"]):
                ffn_tile(last_b, t)


_INS = ['L0_attn_x', 'L0_attn_Wqkv', 'L0_attn_Wout', 'L0_attn_bout', 'L0_ffn_Ws1', 'L0_ffn_Ws2', 'L0_ffn_W1',
        'L0_ffn_W2', 'L0_ffn_Wr']


def rope_tables():
    i = np.arange(DH // 2, dtype=np.float32)
    theta = np.power(np.float32(10000.0), np.float32(-2.0) * (i - np.float32(1.0)) / np.float32(DH))
    angle = np.arange(C, dtype=np.float32)[None, :] * theta[:, None]
    d = (np.arange(P) % (DH * HG)) // HG
    sign = np.where(d % 2 == 0, np.float32(-1.0), np.float32(1.0))
    cos, sin = np.cos(angle)[d // 2], np.sin(angle)[d // 2] * sign[:, None]
    return np.ascontiguousarray(cos, np.float32), np.ascontiguousarray(sin, np.float32)


def kernel(**inputs):
    import numpy as _np
    import concourse.bacc as _bacc
    from concourse import mybir as _mybir
    from concourse.bass_utils import run_bass_kernel_spmd as _run

    nc = _bacc.Bacc("TRN2", target_bir_lowering=False, num_devices=1)
    arrays, args = {}, []
    for name in _INS:
        a = _np.ascontiguousarray(inputs[name])
        arrays[f"in_{name}"] = a
        args.append(nc.dram_tensor(f"in_{name}", a.shape, _mybir.dt.from_np(a.dtype), kind="ExternalInput").ap())
    for name, a in zip(("cos", "sin"), rope_tables()):
        arrays[f"in_{name}"] = a
        args.append(nc.dram_tensor(f"in_{name}", a.shape, _mybir.dt.from_np(a.dtype), kind="ExternalInput").ap())
    args.append(nc.dram_tensor("out_0", (B, C, D), _mybir.dt.float32, kind="ExternalOutput").ap())
    block(nc, *args)
    r = _run(nc, [arrays], core_ids=[0])
    return r.results[0]["out_0"]
```

```python
import concourse.bass as bass
from concourse import mybir
from contextlib import ExitStack
import numpy as np


F32 = mybir.dt.float32
BF16 = mybir.dt.bfloat16
I32 = mybir.dt.int32
ALU = mybir.AluOpType
ACT = mybir.ActivationFunctionType
AXIS_X = mybir.AxisListType.X

B, C, D = 8, 1024, 256
H, DH = 16, 16
HG = 4
G = H // HG
P = 128
NB = C // P
KC = D // P
E, F = 8, 128
HALF = C // 2
PARTS, TERMS = 3, 6
ROWS = TERMS * DH
EPS = 1e-5
SCALE = 1.0 / DH ** 0.5
RING = 3


CHUNKS = [
    [(0, 0, 0, 512, 512), (1, 0, 1, 512, 512)],
    [(0, 0, 2, 512, 512), (1, 0, 3, 512, 512)],
    [(0, 0, 4, 512, 512), (1, 0, 7, 896, 128), (1, 128, 5, 640, 384)],
    [(0, 0, 0, 0, 512), (1, 0, 6, 768, 256), (1, 256, 2, 256, 256)],
    [(0, 0, 1, 128, 384), (0, 384, 3, 384, 128)],
]
DIAGONALS = {2: [(0, 2, 512), (640, 1, 0)], 3: [(0, 2, 512), (768, 1, 0)], 4: [(0, 2, 384)]}
MASKS = {c: len(d) * HG for c, d in DIAGONALS.items()}
MASKS_UNIT = sum(MASKS.values())


def unit_steps():
    steps, dens = [], [("den", j, i) for j in range(HG) for i in range(NB)]
    for c, count in zip(range(5), (7, 7, 6, 6, 6)):
        steps += [("num", c, j) for j in (range(HG) if c < 4 else range(0, HG, 2))]
        steps += [dens.pop(0) for _ in range(count)]
    return steps


STEPS = unit_steps()
NSTEP = len(STEPS)
LAST_STEP = {c: max(s for s, x in enumerate(STEPS) if x[:2] == ("num", c)) for c in range(5)}
FIRST_DEN = next(s for s, x in enumerate(STEPS) if x[0] == "den")

PIECES = [(0, 0), (0, 1), (1, 0), (1, 1), (2, 0), (2, 1), (2, 2), (3, 1), (3, 0), (3, 2), (4, 0), (4, 1)]
PV_STEPS = [
    (6, 11, 21, 22, 30, 32, 34, 39, 42, 43, 47, 49),
    (8, 10, 16, 22, 32, 33, 36, 39, 42, 43, 47, 49),
    (8, 10, 16, 20, 30, 32, 34, 39, 42, 43, 47, 49),
    (7, 10, 17, 20, 30, 32, 37, 39, 42, 43, 47, 49),
]
PV_AT = [dict(zip(steps, PIECES)) for steps in PV_STEPS]
CHUNK_END = [(0, 1), (1, 1), (2, 2), (3, 2), (4, 1)]
Y_FIRST, Y_LAST = [(0, 0), (3, 0)], [(3, 1), (4, 1)]
TAKE_Y = [42, 41, 40, 41]
LOW_LAG = 3
RECIPROCALS = 27

SIDE = [
    {0: ("v", 0), 4: ("v", 1), 9: ("qk", 0), 13: ("v", 2), 16: ("qk", 1), 19: ("qk", 2), 26: ("qk", 3),
     28: ("v", 3)},
    {0: ("qk", 0), 7: ("qk", 1), 11: ("qk", 2), 18: ("qk", 3), 24: ("norm", 0), 26: ("norm", 1),
     28: ("acc", 0), 29: ("acc", 1), 35: ("acc", 2), 38: ("acc", 3)},
    {0: ("qk", 0), 5: ("t2", 0), 7: ("qk", 1), 8: ("t2", 1), 11: ("qk", 2), 15: ("t2", 2), 17: ("qk", 3),
     19: ("t2", 3), 24: ("route", 0), 25: ("route", 1), 28: ("norm", 0), 31: ("norm", 1), 35: ("acc", 0),
     37: ("acc", 1), 39: ("route", 2), 41: ("acc", 2), 44: ("acc", 3)},
    {0: ("xt", 0), 3: ("xt", 1), 5: ("xt", 2), 8: ("xt", 3), 11: ("qk", 0), 16: ("ffn", 0), 18: ("qk", 1),
     21: ("ffn", 1), 23: ("qk", 2), 28: ("ffn", 2), 31: ("qk", 3), 34: ("ffn", 3), 36: ("ffn", 4),
     38: ("ffn", 5), 41: ("ffn", 6), 45: ("ffn", 7)},
]
IN_TWO = {("v", 0), ("v", 1), ("v", 2), ("v", 3), ("qk", 0), ("qk", 2)}
FFN = [("up", 0), ("up", 1), ("down", 0), ("up", 2), ("down", 1), ("up", 3), ("down", 2), ("down", 3)]
PAIR_OF = {1: 1, 2: 0}
LAST_TILES = [("route", 0), ("ffn", 0), ("ffn", 1), ("route", 1), ("ffn", 2), ("ffn", 3), ("route", 2),
              ("ffn", 4), ("ffn", 5), ("ffn", 6), ("ffn", 7)]
TILES = {"v": 4, "xt": 4, "qk": 4 * G, "norm": 4, "acc": 8, "t2": 4, "route": 3, "ffn": 8, "gen": 12 * E}
STATS2 = (1, 44)
STATS1 = {(1, 47): 0, (2, 7): 1, (2, 11): 2, (2, 14): 3, (2, 48): 4}
COPY = (1, 44)
GAP = (2, 36)
BRANCH = (3, 10)


def runs(kind, g, first, last):
    if first and (kind in ("t2", "route", "ffn") or kind in ("norm", "acc") and PAIR_OF[g] == 1):
        return False
    return not (last and (kind == "xt" or kind == "qk" and g == G - 1))


def block(nc, x, w_qkv, w_out, b_out, ws1, ws2, w1, w2, wr, cos_in, sin_in, out):
    x_v = x.rearrange("b (n p) d -> b p n d", p=P)
    out_v = out.rearrange("b (n p) d -> b p n d", p=P)
    scratch = nc.dram_tensor("qk_parts", (2, PARTS, 2, DH * HG, C), BF16, kind="Internal").ap()

    with ExitStack() as ctx:
        def sb(name, shape, dt=F32):
            return ctx.enter_context(nc.sbuf_tensor(name, shape, dt))

        def ps(name, shape):
            return ctx.enter_context(nc.psum_tensor(name, shape, F32))

        def sem(name):
            return ctx.enter_context(nc.semaphore(name))

        stack = sb("stack", [P, 2, 2, 2, HG * C], BF16)
        probs = sb("probs", [P, 2, HG, C])
        x_in = sb("x_in", [P, NB, D])
        xn = sb("xn", [P, 2, 2, D])
        xnt = sb("xnt", [P, KC, C])
        v_sb = sb("v_sb", [P, NB, H, 2, DH])
        x_acc = sb("x_acc", [P, NB, D])
        x_mid = sb("x_mid", [P, NB, D])
        y_sb = sb("y_sb", [P, 2, C])
        w_qk = sb("w_qk", [P, KC, G, P])
        swap = sb("swap", [P, P], BF16)
        w_v = sb("w_v", [P, KC, D])
        w_o = sb("w_o", [P, 2, D])
        ws1_sb = sb("ws1_sb", [P, KC, F])
        ws2_sb = sb("ws2_sb", [P, D])
        wr_sb = sb("wr_sb", [P, KC, 32])
        cos_sb = sb("cos_sb", [P, C])
        sin_sb = sb("sin_sb", [P, C])
        bias = sb("bias", [P, D])
        ident = sb("ident", [P, P])
        ones = sb("ones", [P, P])
        parts = sb("parts", [P, 2, PARTS, HALF], BF16)
        rest = sb("rest", [P, HALF])
        raw = sb("raw", [P, HALF])
        rot = sb("rot", [P, HALF])
        den = sb("den", [P, 2, NB, HG])
        rden = sb("rden", [P, NB, 2, HG])
        spread = [rest[:, :], rot[:, :]]
        stats = sb("stats", [P, NB, 6])
        mean_var = sb("mean_var", [P, 2, NB, 2])
        rstd = sb("rstd", [P, 2, NB])
        root = [sb(f"root{i}", [P, NB]) for i in range(3)]
        xn2t = sb("xn2t", [P, KC, C])
        hidden = sb("hidden", [P, 2 * P])
        hidden2 = sb("hidden2", [P, 2, 2 * P])
        logits_t = sb("logits_t", [P, 2 * P])
        logits = sb("logits", [P, NB, E])
        top = sb("top", [P, NB, 8])
        gap = sb("gap", [P, NB])
        gap_exp = sb("gap_exp", [P, NB])
        weight = sb("weight", [P, NB])
        prob = sb("prob", [P, NB, E])
        routed = sb("routed", [1, 1])
        routed_i = sb("routed_i", [1, 1], I32)
        gate = sb("gate", [P, 2 * P])
        w1_now = sb("w1_now", [P, KC, F])
        w2_now = sb("w2_now", [P, D])

        scores = ps("scores", [P, RING, 2 * HALF])
        y_ps = ps("y_ps", [P, HALF])
        side = ps("side", [P, HALF])[:, :]

        loaded = sem("loaded")
        tables_loaded = sem("tables_loaded")
        more_loaded = sem("more_loaded")
        consts = sem("consts")
        weights_ready = sem("weights_ready")
        x_loaded = sem("x_loaded")
        plain_sent = sem("plain_sent")
        rot_sent = sem("rot_sent")
        stacked = [sem("stacked0"), sem("stacked1")]
        out_sent = sem("out_sent")
        scores_ready = sem("scores_ready")
        exp_done = sem("exp_done")
        masked = sem("masked")
        chunk_used = sem("chunk_used")
        y_ready = sem("y_ready")
        y_taken = sem("y_taken")
        spread_ready = sem("spread_ready")
        den_used = sem("den_used")
        full = {k: sem(f"{k}_full") for k in TILES}
        taken = {k: sem(f"{k}_taken") for k in TILES}
        xn_ready = sem("xn_ready")
        xn2_ready = sem("xn2_ready")
        raw_ready = sem("raw_ready")
        middle_ready = sem("middle_ready")
        low_ready = sem("low_ready")
        x_acc_used = sem("x_acc_used")
        x_copied = sem("x_copied")
        gap_ready = sem("gap_ready")
        gap_exped = sem("gap_exped")
        weight_ready = sem("weight_ready")
        hidden_ready = sem("hidden_ready")
        routed_ready = sem("routed_ready")
        expert_loaded = sem("expert_loaded")
        gate_ready = sem("gate_ready")
        out_ready = sem("out_ready")

        program = ctx.enter_context(nc.Block())
        MORE_LOADS = 13

        held = {e: sem(f"held_{e}") for e in ("sp", "pool", "pe", "dve")}

        def at1(b, per, k):
            return b * per + k + 1

        def score_tile(n):
            return scores[:, n % RING, :]

        def bank(n):
            n %= 2 * RING
            return scores[:, n // 2, n % 2 * HALF:(n % 2 + 1) * HALF]

        def at(b, per, k):
            return b * per + k

        stage = probs[:, 0, 0, 0:KC * 2 * D].rearrange("p (k n) -> p k n", k=KC)

        @program.sync
        def _(sp):
            w_qkv_v = w_qkv.rearrange("(k p) n -> p k n", p=P)
            sp.dma_start(x_in[:, :, :], x_v[0]).then_inc(x_loaded, 16)
            sp.dma_start(stage, w_qkv_v[:, :, 0:2 * D]).then_inc(loaded, 16)
            sp.dma_start(cos_sb[:, :], cos_in).then_inc(tables_loaded, 16)
            sp.dma_start(sin_sb[:, :], sin_in).then_inc(tables_loaded, 16)
            sp.dma_start(w_v[:, :, :], w_qkv_v[:, :, 2 * D:3 * D]).then_inc(more_loaded, 16)
            wo_v = w_out.rearrange("(p a j d) n -> a j d p n", p=2, a=2, j=HG)
            for a in range(2):
                for j in range(HG):
                    sp.dma_start(w_o[32 * j + DH * a:32 * j + DH * (a + 1), :, :], wo_v[a, j]).then_inc(more_loaded, 16)
            sp.dma_start(bias[:, :], b_out.rearrange("(a n) -> a n", a=1).to_broadcast([P, D])).then_inc(more_loaded, 16)
            sp.dma_start(ws1_sb[:, :, :], ws1.rearrange("(k p) f -> p k f", p=P)).then_inc(more_loaded, 16)
            sp.dma_start(ws2_sb[:, :], ws2).then_inc(more_loaded, 16)
            sp.dma_start(wr_sb[:, :, 0:E], wr.rearrange("(k p) e -> p k e", p=P)).then_inc(more_loaded, 16)

            def send_parts(b, g, outs=None):
                parity = g % 2
                if not (isinstance(b, int) and b == 0 and g == 0):
                    sp.wait_ge(stacked[1 - parity], at(b, 2 * 12 * 16, (g + parity) // 2 * 12 * 16))
                    sp.sem_inc(held["sp"], 1)
                for half in range(2):
                    for kind, sent in ((0, plain_sent), (1, rot_sent)):
                        sp.wait_ge(low_ready, at(b, 16, 4 * g + 2 * half + kind + 1))
                        sp.sem_inc(held["sp"], 1)
                        sp.dma_start(scratch[kind, :, :, :, half * HALF:(half + 1) * HALF].rearrange("c s r t -> (s r) c t"),
                                     parts[:, kind, :, :]).then_inc(sent, 16)
                        if half == 1:
                            if kind == 0 and not (isinstance(b, int) and b == 0 and g < 2):
                                sp.wait_ge(scores_ready, at(b, G * NSTEP, (g - 1) * NSTEP))
                                sp.sem_inc(held["sp"], 1)
                            fill_stacks(b, g, kind, sent)
                    if outs is not None:
                        send_out(outs, half)

            def fill_stacks(b, g, kind, sent):
                parity = g % 2
                sp.wait_ge(sent, at(b, 8 * 16, 2 * 16 * (g + 1)))
                sp.sem_inc(held["sp"], 1)
                src = scratch[kind].rearrange("c s (d h) t -> c s d (h t)", h=HG)
                row = 0
                for part, copies in ((0, 3), (1, 2), (2, 1)):
                    s = src[part, 0]
                    if copies > 1:
                        s = s.unsqueeze(0).to_broadcast([copies, DH, HG * C])
                    sp.dma_start(stack[row:row + copies * DH, parity, kind, 0, :], s).then_inc(stacked[parity], 16)
                    row += copies * DH
                row = 0
                for n in (3, 2, 1):
                    sp.dma_start(stack[row:row + n * DH, parity, kind, 1, :], src[0:n, 1]).then_inc(stacked[parity], 16)
                    row += n * DH

            def batch(b, first, last):
                for g in range(G):
                    if g < G - 1:
                        send_parts(b, g + 1)
                    elif not last:
                        send_parts(b + 1, 0, None if first else b - 1)
                    if g == 1 and not last:
                        sp.wait_ge(x_copied, at(b, 1, 1))
                        sp.sem_inc(held["sp"], 1)
                        sp.dma_start(x_in[:, :, :], x_v[b + 1]).then_inc(x_loaded, 16)
                if not first:
                    for pair in range(0 if last else 2, G):
                        send_out(b - 1, pair)

            def send_out(b, g):
                sp.wait_ge(out_ready, at(b, G, g + 1))
                sp.sem_inc(held["sp"], 1)
                sp.dma_start(out_v[b][:, 2 * g:2 * g + 2, :], x_mid[:, 2 * g:2 * g + 2, :]).then_inc(out_sent, 16)

            sp.sem_inc(out_sent, 1)
            send_parts(0, 0)
            batch(0, True, False)
            with sp.Fori(1, B - 1) as b:
                batch(b, False, False)
            batch(B - 1, False, True)
            sp.wait_ge(taken["gen"], at1(B - 1, TILES["gen"], TILES["gen"]))
            for g in range(G):
                send_out(B - 1, g)
            sp.wait_ge(out_sent, at1(B, 16 * G, 0))

        @program.gpsimd
        def _(pool):
            nc.gpsimd.memset(ones[:, :], 1.0).then_inc(consts, 1)
            nc.gpsimd.memset(wr_sb[:, :, E:32], 0.0).then_inc(consts, 1)
            nc.gpsimd.memset(ident[:, :], 0.0).then_inc(consts, 1)
            nc.gpsimd.memset(swap[:, :], 0.0).then_inc(consts, 1)
            nc.gpsimd.memset(v_sb[:, :, :, :, :], 0.0).then_inc(consts, 1)
            pool.wait_ge(consts, 5)
            swap_v = swap[:, :].rearrange("p (u w v) -> p w u v", w=2, v=HG)
            for w in range(2):
                nc.gpsimd.affine_select(out=swap_v[:, w], in_=swap_v[:, w], compare_op=ALU.not_equal, fill=1.0,
                                        base=-HG * (1 - w), pattern=[[-2 * HG, P // (2 * HG)], [-1, HG]],
                                        channel_multiplier=1).then_inc(consts, 1)
            nc.gpsimd.affine_select(out=ident[:, :], in_=ident[:, :], compare_op=ALU.not_equal, fill=1.0, base=0,
                                    pattern=[[-1, P]], channel_multiplier=1).then_inc(consts, 1)

            def mask(b, g, c):
                for j in range(HG):
                    step = LAST_STEP[c] - (HG - 1 - j if c < 4 else 1 - j // 2)
                    pool.wait_ge(exp_done, at(b, G * NSTEP, g * NSTEP + step + 1))
                    pool.sem_inc(held["pool"], 1)
                    for col, n, stride in DIAGONALS[c]:
                        p = probs[:, (5 * g + c) % 2, j, :]
                        if n == 1:
                            v, pattern = p[:, col:col + P], [[1, P]]
                        else:
                            v = p[:, col:col + n * stride].rearrange("p (n s) -> p n s", n=n)[:, :, 0:P]
                            pattern = [[0, n], [1, P]]
                        nc.gpsimd.affine_select(out=v, in_=v, compare_op=ALU.is_ge, fill=0.0, base=0,
                                                pattern=pattern, channel_multiplier=-1).then_inc(masked, 1)

            def low_part(b, g, t):
                if t % 2 == 0:
                    pool.wait_ge(raw_ready, at(b, 8, 2 * g + t // 2 + 1))
                    nc.gpsimd.tensor_tensor(rot[:, :], raw[:, :], cos_sb[:, t // 2 * HALF:(t // 2 + 1) * HALF], ALU.mult)
                pool.wait_ge(middle_ready, at(b, 16, 4 * g + t + 1))
                nc.gpsimd.tensor_tensor(parts[:, t % 2, 2, :], rest[:, :], parts[:, t % 2, 1, :], ALU.subtract
                                        ).then_inc(low_ready, 1)

            def load_experts(b):
                pool.wait_ge(routed_ready, at(b, 1, 1))
                pool.sem_inc(held["pool"], 1)
                count = pool.value_load(routed_i[0:1, 0:1], min_val=0, max_val=C)
                with pool.If(count > 0):
                    with pool.Fori(0, E) as e:
                        pool.wait_ge(taken["gen"], at1(b, TILES["gen"], 0) + e * 12)
                        pool.sem_inc(held["pool"], 1)
                        pool.dma_start(w1_now[:, :, :], w1[bass.ds(e, 1)].rearrange("e (k p) f -> p (e k) f", p=P)
                                       ).then_inc(expert_loaded, 16)
                        pool.dma_start(w2_now[:, :], w2[bass.ds(e, 1)].rearrange("e f d -> f (e d)")
                                       ).then_inc(expert_loaded, 16)
                with pool.Else():
                    pool.sem_inc(expert_loaded, 32 * E)

            def batch(b, first, last):
                for g in range(G):
                    for s in range(NSTEP):
                        if (g, s) == COPY:
                            if not first:
                                pool.wait_ge(x_acc_used, at(b, 1, 0))
                            else:
                                pool.wait_ge(x_loaded, 16)
                            nc.gpsimd.tensor_tensor(x_acc[:, :, :], x_in[:, :, :],
                                                    bias[:, :].unsqueeze(1).to_broadcast([P, NB, D]), ALU.add
                                                    ).then_inc(x_copied, 1)
                        for c in DIAGONALS:
                            if s == LAST_STEP[c] + 1:
                                mask(b, g, c)
                        kind, t = SIDE[g].get(s - LOW_LAG, ("none", 0))
                        if kind == "qk" and runs("qk", g, first, last):
                            b1, g1 = (b, g + 1) if g < G - 1 else (b + 1, 0)
                            low_part(b1, g1, t)
                        if (g, s) == BRANCH and not first:
                            load_experts(b - 1)

            pool.wait_ge(loaded, 16)
            for k in range(KC):
                for g in range(G):
                    for a in range(2):
                        src = stage[:, k, a * D + g * HG * DH:a * D + (g + 1) * HG * DH].rearrange("p (h d) -> p d h", d=DH)
                        dst = w_qk[:, k, g, a * HG * DH:(a + 1) * HG * DH].rearrange("p (d h) -> p d h", h=HG)
                        last = nc.gpsimd.tensor_copy(dst, src)
            last.then_inc(weights_ready, 1)
            pool.wait_ge(tables_loaded, 32)
            for t in range(4):
                low_part(0, 0, t)
            pool.wait_ge(more_loaded, 16 * MORE_LOADS)
            batch(0, True, False)
            with pool.Fori(1, B - 1) as b:
                batch(b, False, False)
            batch(B - 1, False, True)
            load_experts(B - 1)

        @program.scalar
        def _(act):
            def batch(b, first):
                for g in range(G):
                    for s, step in enumerate(STEPS):
                        act_step(b, first, g, s, step)
                        if (g, s) == GAP and not first:
                            exp_gap(b - 1)

            def act_step(b, first, g, s, step):
                n = g * NSTEP + s
                act.wait_ge(scores_ready, at(b, G * NSTEP, n + 1))
                src = score_tile(n)
                if step[0] == "den":
                    _, j, i = step
                    if s == FIRST_DEN and not (first and g < 2):
                        act.wait_ge(den_used, at(b, G, g - 1))
                    nc.scalar.activation(src, src, ACT.Exp, scale=SCALE,
                                         accum_out=den[:, g % 2, i, j:j + 1]).then_inc(exp_done, 1)
                    return
                _, c, j = step
                chunk = 5 * g + c
                if j == 0 and not (first and chunk < 2):
                    act.wait_ge(chunk_used, at(b, 5 * G, chunk - 1))
                if j == 0 and first and chunk < 2:
                    act.wait_ge(weights_ready, 1)
                if c < 4:
                    nc.scalar.activation(probs[:, chunk % 2, j, :], src, ACT.Exp, scale=SCALE).then_inc(exp_done, 1)
                else:
                    nc.scalar.activation(probs[:, chunk % 2, j:j + 2, 0:HALF], src.rearrange("p (a n) -> p a n", a=2),
                                         ACT.Exp, scale=SCALE).then_inc(exp_done, 1)

            def exp_gap(b):
                act.wait_ge(gap_ready, at(b, 1, 1))
                nc.scalar.activation(gap_exp[:, :], gap[:, :], ACT.Exp).then_inc(gap_exped, 1)

            batch(0, True)
            with act.Fori(1, B) as b:
                batch(b, False)
            exp_gap(B - 1)

        @program.tensor
        def _(pe):
            pe.wait_ge(consts, 8)

            def scores_step(b, first, g, s, step):
                n = g * NSTEP + s
                if n >= RING:
                    pe.wait_ge(exp_done, at(b, G * NSTEP, n - RING + 1))
                elif not first:
                    user = max(m for m in range(G * NSTEP) if m % RING == n)
                    pe.wait_ge(exp_done, at(b - 1, G * NSTEP, user + 1))
                tile = score_tile(n)
                q, k = (stack[0:ROWS, g % 2, 0 if step[0] == "den" else 1, a, :].rearrange("p (h t) -> p h t", h=HG)
                        for a in (0, 1))
                if step[0] == "den":
                    _, j, i = step
                    for half in range(2):
                        mm = nc.tensor.matmul(tile[:, half * HALF:(half + 1) * HALF], q[:, j, i * P:(i + 1) * P],
                                              k[:, j, half * HALF:(half + 1) * HALF], start=True, stop=True)
                else:
                    _, c, j = step
                    for h in ((j,) if c < 4 else (j, j + 1)):
                        for bank, col, i, q0, n in CHUNKS[c]:
                            col += (bank + h - j) * HALF
                            mm = nc.tensor.matmul(tile[:, col:col + n], k[:, h, i * P:(i + 1) * P], q[:, h, q0:q0 + n],
                                                  start=True, stop=True)
                mm.then_inc(scores_ready, 1)

            def heads_step(b, first, g, s):
                piece = PV_AT[g][s]
                c = piece[0]
                bank, col, i, q0, n = CHUNKS[c][piece[1]]
                col += bank * HALF
                if piece in Y_FIRST and not (first and g == 0 and c == 0):
                    pe.wait_ge(y_taken, at(b, 2 * G, 2 * g + Y_FIRST.index(piece)))
                if g == 0:
                    pe.wait_ge(taken["v"], at(b, 4, i // 2 + 1))
                if c in MASKS:
                    done = sum(m for k, m in MASKS.items() if k <= c)
                    pe.wait_ge(masked, at(b, G * MASKS_UNIT, g * MASKS_UNIT + done))
                else:
                    pe.wait_ge(exp_done, at(b, G * NSTEP, g * NSTEP + LAST_STEP[c] + 1))
                o0 = q0 % HALF
                for j in range(HG):
                    h = g * HG + j
                    mm = nc.tensor.matmul(y_ps[32 * j:32 * j + 32, o0:o0 + n], v_sb[:, i, h, :, :],
                                          probs[:, (5 * g + c) % 2, j, col:col + n], start=piece in Y_FIRST, stop=piece in Y_LAST,
                                          tile_position=(0, 32 * j), skip_group_check=True)
                if piece in CHUNK_END:
                    mm.then_inc(chunk_used, 1)
                elif piece in Y_LAST:
                    mm.then_inc(y_ready, 1)

            def v_tile(b, t, i):
                for k in range(KC):
                    mm = nc.tensor.matmul(side[:, i * D:(i + 1) * D], xnt[:, k, (2 * t + i) * P:(2 * t + i + 1) * P],
                                          w_v[:, k, :], start=k == 0, stop=k == KC - 1)
                if i == 1:
                    mm.then_inc(full["v"], 1)

            def xt_tile(b, t, side=side):
                pe.wait_ge(xn_ready, at(b, 4, t + 1))
                for k in range(KC):
                    for i in range(2):
                        mm = nc.tensor.transpose(side[:, (2 * k + i) * P:(2 * k + i + 1) * P], xn[:, t % 2, i, k * P:(k + 1) * P],
                                                 ident[:, :])
                mm.then_inc(full["xt"], 1)

            def qk_tile(b, g, t, k, side=side):
                half = t // 2
                if t % 2 == 0:
                    if t == 0 and k == 0 and g == 0:
                        pe.wait_ge(taken["xt"], at(b, 4, 4))
                    mm = nc.tensor.matmul(side, w_qk[:, k, g, :], xnt[:, k, half * HALF:(half + 1) * HALF],
                                          start=k == 0, stop=k == KC - 1)
                    if k == 0:
                        return
                else:
                    pe.wait_ge(low_ready, at(b, 16, 4 * g + t))
                    for i in range(PARTS):
                        mm = nc.tensor.matmul(side, swap[:, :], parts[:, 0, i, :], start=i == 0, stop=i == PARTS - 1)
                mm.then_inc(full["qk"], 1)

            def norm_tile(b, pair, t, side=side):
                pe.wait_ge(spread_ready, at(b, 4, 2 * pair + t + 1))
                for i in range(NB // 2):
                    mm = nc.tensor.transpose(side[:, i * P:(i + 1) * P], spread[t][:, i * P:(i + 1) * P], ident[:, :])
                mm.then_inc(full["norm"], 1)

            def acc_tile(b, pair, t, side=side):
                if t == 0:
                    pe.wait_ge(taken["norm"], at(b, 4, 2 * pair + 2))
                for i in range(2):
                    mm = nc.tensor.matmul(side[:, i * D:(i + 1) * D], y_sb[:, pair, (2 * t + i) * P:(2 * t + i + 1) * P],
                                          w_o[:, pair, :], start=True, stop=True)
                mm.then_inc(full["acc"], 1)

            def t2_tile(b, t, side=side):
                pe.wait_ge(xn2_ready, at(b, 4, t + 1))
                for k in range(KC):
                    for i in range(2):
                        mm = nc.tensor.transpose(side[:, (2 * k + i) * P:(2 * k + i + 1) * P], xn[:, t % 2, i, k * P:(k + 1) * P],
                                                 ident[:, :])
                mm.then_inc(full["t2"], 1)

            def route_tile(b, t, side=side):
                if t == 0:
                    pe.wait_ge(taken["t2"], at(b, 4, 4))
                    for k in range(KC):
                        for j in range(4):
                            mm = nc.tensor.matmul(side[32 * j:32 * j + 32, 0:2 * P], wr_sb[:, k, :],
                                                  xn2t[:, k, 2 * j * P:2 * (j + 1) * P], start=k == 0, stop=k == KC - 1,
                                                  tile_position=(0, 32 * j), skip_group_check=True)
                elif t == 1:
                    pe.wait_ge(taken["route"], at(b, TILES["route"], 1))
                    for i in range(2):
                        mm = nc.tensor.transpose(side[:, i * P:(i + 1) * P], logits_t[:, i * P:(i + 1) * P], ident[:, :])
                else:
                    pe.wait_ge(weight_ready, at(b, 1, 1))
                    mm = nc.tensor.matmul(side[:, 0:NB], ones[:, :], weight[:, :], start=True, stop=True)
                mm.then_inc(full["route"], 1)

            def ffn_tile(b, t, side=side):
                what, pair = FFN[t]
                if what == "up":
                    for k in range(KC):
                        mm = nc.tensor.matmul(side[:, 0:2 * P], ws1_sb[:, k, :], xn2t[:, k, 2 * pair * P:2 * (pair + 1) * P],
                                              start=k == 0, stop=k == KC - 1)
                else:
                    pe.wait_ge(hidden_ready, at(b, 4, pair + 1))
                    for i in range(2):
                        mm = nc.tensor.matmul(side[:, i * D:(i + 1) * D], hidden2[:, pair % 2, i * P:(i + 1) * P], ws2_sb[:, :],
                                              start=True, stop=True)
                mm.then_inc(full["ffn"], 1)

            def experts(b):
                pe.wait_ge(routed_ready, at(b, 1, 1))
                pe.sem_inc(held["pe"], 1)
                count = pe.value_load(routed_i[0:1, 0:1], min_val=0, max_val=C)
                with pe.If(count > 0):
                    with pe.Fori(0, E) as e:
                        base = at1(b, TILES["gen"], 0) + e * 12
                        pe.wait_ge(expert_loaded, at(b, 32 * E, 32) + e * 32)
                        pe.sem_inc(held["pe"], 1)
                        for pair in range(4):
                            pe.wait_ge(gate_ready, at(b, 4 * E, pair + 1) + e * 4)
                            pe.wait_ge(taken["gen"], base + 3 * pair)
                            for i in range(2):
                                mm = nc.tensor.transpose(side[:, i * P:(i + 1) * P], gate[:, i * P:(i + 1) * P], ident[:, :])
                            mm.then_inc(full["gen"], 1)
                            pe.wait_ge(taken["gen"], base + (3 * pair + 1))
                            for k in range(KC):
                                mm = nc.tensor.matmul(side[:, 0:2 * P], w1_now[:, k, :], xn2t[:, k, 2 * pair * P:2 * (pair + 1) * P],
                                                      start=k == 0, stop=k == KC - 1)
                            mm.then_inc(full["gen"], 1)
                            pe.wait_ge(taken["gen"], base + (3 * pair + 2))
                            for i in range(2):
                                mm = nc.tensor.matmul(side[:, i * D:(i + 1) * D], hidden[:, i * P:(i + 1) * P], w2_now[:, :],
                                                      start=True, stop=True)
                            mm.then_inc(full["gen"], 1)
                with pe.Else():
                    pe.sem_inc(full["gen"], TILES["gen"])

            def tile_of(b, g, kind, t):
                if kind == "qk":
                    return (b, 4 * (g + 1) + t) if g < G - 1 else (b + 1, t)
                if kind in ("norm", "acc"):
                    pair = PAIR_OF[g]
                    return b - pair, TILES[kind] // 2 * pair + t
                return (b if kind == "v" else b + 1 if kind == "xt" else b - 1), t

            def side_step(b, first, last, g, s, before):
                second = (s - 1) in SIDE[g] and SIDE[g][s - 1] in IN_TWO
                if not second and s not in SIDE[g]:
                    return before
                kind, t = SIDE[g][s - 1 if second else s]
                if not runs(kind, g, first, last):
                    return before
                bb, n = tile_of(b, g, kind, t)
                if not second:
                    for k0, b0, n0 in before:
                        pe.wait_ge(taken[k0], (at1 if k0 in ("ffn", "gen") else at)(b0, TILES[k0], n0 + 1))
                if kind == "v":
                    v_tile(bb, t, int(second))
                elif kind == "xt":
                    xt_tile(bb, t)
                elif kind == "qk":
                    qk_tile(bb, n // 4, t, int(second))
                elif kind == "norm":
                    norm_tile(bb, n // 2, t)
                elif kind == "acc":
                    acc_tile(bb, n // 4, t)
                elif kind == "t2":
                    t2_tile(bb, t)
                elif kind == "route":
                    route_tile(bb, t)
                else:
                    ffn_tile(bb, t)
                return [(kind, bb, n)]

            def batch(b, first, last):
                before = [("qk", b, 3)] + ([] if first else [("ffn", b - 2, TILES["ffn"] - 1)])
                for g in range(G):
                    parity = g % 2
                    pe.wait_ge(stacked[parity], at(b, 2 * 12 * 16, (g // 2 + 1) * 12 * 16))
                    for s, step in enumerate(STEPS):
                        scores_step(b, first, g, s, step)
                        if s in PV_AT[g]:
                            heads_step(b, first, g, s)
                        before = side_step(b, first, last, g, s, before)
                        if (g, s) == BRANCH and not first:
                            for k0, b0, n0 in before:
                                pe.wait_ge(taken[k0], at(b0, TILES[k0], n0 + 1))
                            experts(b - 1)
                            before = before + [("gen", b - 1, TILES["gen"] - 1)]

            for t in range(4):
                xt_tile(0, t, bank(t))
            pe.wait_ge(weights_ready, 1)
            for t in range(4):
                for k in range(KC if t % 2 == 0 else 1):
                    qk_tile(0, 0, t, k, bank(4 + t))
            pe.wait_ge(more_loaded, 16 * MORE_LOADS)
            batch(0, True, False)
            with pe.Fori(1, B - 1) as b:
                batch(b, False, False)
            batch(B - 1, False, True)
            last = B - 1
            for t in range(2):
                norm_tile(last, 1, t, bank(t))
            for t in range(4):
                acc_tile(last, 1, t, bank(2 + t))
            for t in range(4):
                t2_tile(last, t, bank(t))
            pe.wait_ge(taken["t2"], at(last, 4, 4))
            for n, (kind, t) in enumerate(LAST_TILES):
                if n >= 4:
                    k0, t0 = LAST_TILES[n - 4]
                    pe.wait_ge(taken[k0], (at1 if k0 == "ffn" else at)(last, TILES[k0], t0 + 1))
                (route_tile if kind == "route" else ffn_tile)(last, t, bank(n % 4))
            pe.wait_ge(taken["ffn"], at1(last - 1, TILES["ffn"], TILES["ffn"]))
            experts(last)

        @program.vector
        def _(dve):
            def settle():
                dve.drain()

            def inverse_root(n, var, result):
                v, a, y = (r[:, 0:n] for r in root)
                nc.vector.tensor_scalar(v, var, EPS, None, ALU.add)
                settle()
                nc.vector.tensor_scalar(a.bitcast(I32), v.bitcast(I32), 1, None, ALU.logical_shift_right)
                settle()
                nc.vector.tensor_scalar(y.bitcast(I32), a.bitcast(I32), -1.0, float(0x5f3759df), ALU.mult, ALU.add)
                settle()
                for i in range(3):
                    nc.vector.scalar_tensor_tensor(a, y, -0.5, y, ALU.mult, ALU.mult)
                    settle()
                    nc.vector.tensor_tensor(a, a, v, ALU.mult)
                    settle()
                    nc.vector.scalar_tensor_tensor(result if i == 2 else y, a, 1.5, y, ALU.add, ALU.mult)
                    settle()

            def block_stats(src, t):
                for i in (2 * t, 2 * t + 1):
                    nc.vector.bn_stats(stats[:, i, :], src[:, i, :])

            def layernorm_stats(which):
                settle()
                for i in range(NB):
                    nc.vector.bn_aggr(mean_var[:, which, i, :], stats[:, i, :])
                settle()
                inverse_root(NB, mean_var[:, which, :, 1], rstd[:, which, :])

            def layernorm(src, which, t, ready):
                for i in range(2):
                    blk = 2 * t + i
                    last = nc.vector.tensor_scalar(xn[:, t % 2, i, :], src[:, blk, :], mean_var[:, which, blk, 0:1],
                                                   rstd[:, which, blk:blk + 1], ALU.subtract, ALU.mult)
                last.then_inc(ready, 1)

            def v_tile(b, first, t):
                if t == 0 and not first:
                    dve.wait_ge(chunk_used, at(b, 5 * G, 0))
                dve.wait_ge(full["v"], at(b, 4, t + 1))
                for a in range(2):
                    src = side.rearrange("p (i q a c) -> p i q a c", i=2, a=2, c=HG * DH)[:, :, :, a, :]
                    for i in range(2):
                        last = nc.vector.tensor_copy(
                            v_sb[:, 2 * t + i, :, a, :].rearrange("p (q a h) d -> p q a h d", a=2, h=HG)[:, :, a],
                            src[:, i].rearrange("p q (h d) -> p q h d", d=DH))
                last.then_inc(taken["v"], 1)

            def xt_tile(b, t, side=side):
                dve.wait_ge(full["xt"], at(b, 4, t + 1))
                nc.vector.tensor_copy(xnt[:, :, 2 * t * P:(2 * t + 2) * P], side.rearrange("p (k n) -> p k n", k=KC)
                                      ).then_inc(taken["xt"], 1)
                if t < 2:
                    layernorm(x_in, 0, t + 2, xn_ready)

            def split(kind, src):
                nc.vector.tensor_copy(parts[:, kind, 0, :], src)
                settle()
                nc.vector.tensor_tensor(rest[:, :], src, parts[:, kind, 0, :], ALU.subtract)

            def middle(kind):
                settle()
                nc.vector.tensor_copy(parts[:, kind, 1, :], rest[:, :]).then_inc(middle_ready, 1)

            def qk_tile(b, g, t, very_first, side=side):
                half = t // 2
                cols = slice(half * HALF, (half + 1) * HALF)
                dve.wait_ge(full["qk"], at(b, 16, 4 * g + t + 1))
                if not (very_first and half == 0):
                    dve.wait_ge((plain_sent, rot_sent)[t % 2], at(b, 8 * 16, 16 * (2 * g + half)))
                if t % 2 == 0:
                    if not (very_first and t == 0):
                        dve.wait_ge(low_ready, at(b, 16, 4 * g + t))
                    nc.vector.tensor_copy(raw[:, :], side).then_inc(taken["qk"], 1)
                    dve.drain().then_inc(raw_ready, 1)
                    split(0, raw[:, :])
                    middle(0)
                else:
                    dve.wait_ge(low_ready, at(b, 16, 4 * g + t))
                    nc.vector.tensor_tensor(rest[:, :], side, sin_sb[:, cols], ALU.mult).then_inc(taken["qk"], 1)
                    settle()
                    nc.vector.tensor_tensor(rot[:, :], rot[:, :], rest[:, :], ALU.add)
                    settle()
                    split(1, rot[:, :])
                    middle(1)

            def reciprocals(b, g):
                dve.wait_ge(exp_done, at(b, G * NSTEP, (g + 1) * NSTEP))
                nc.vector.reciprocal(rden[:, :, g % 2, :], den[:, g % 2, :, :]).then_inc(den_used, 1)
                settle()

            def spread_reciprocals(lows):
                dve.wait_ge(low_ready, lows)
                for t in range(2):
                    blocks = slice((1 - t) * NB // 2, (2 - t) * NB // 2)
                    for a in range(2):
                        last = nc.vector.tensor_copy(
                            spread[t].rearrange("p (i h a r) -> p i h a r", h=HG, a=2, r=DH)[:, :, :, a, :],
                            rden[:, blocks, a, :].unsqueeze(3).to_broadcast([P, NB // 2, HG, DH]))
                    last.then_inc(spread_ready, 1)

            def take_y(b, g, t):
                if t == 0:
                    dve.wait_ge(y_ready, at(b, G, g + 1))
                else:
                    dve.wait_ge(chunk_used, at(b, 5 * G, 5 * (g + 1)))
                y = y_sb[:, g // 2, (1 - t) * HALF:(2 - t) * HALF]
                if g % 2 == 0:
                    nc.vector.tensor_copy(y, y_ps[:, :]).then_inc(y_taken, 1)
                else:
                    nc.vector.tensor_tensor(y, y_ps[:, :], y, ALU.add).then_inc(y_taken, 1)
                settle()

            def norm_tile(b, pair, t, side=side):
                dve.wait_ge(full["norm"], at(b, 4, 2 * pair + t + 1))
                y = y_sb[:, pair, (1 - t) * HALF:(2 - t) * HALF]
                nc.vector.tensor_tensor(y, side, y, ALU.mult).then_inc(taken["norm"], 1)

            def acc_tile(b, pair, t, side=side):
                if pair == 0 and t == 0:
                    dve.wait_ge(x_copied, at(b, 1, 1))
                if pair == 1 and t == 0:
                    dve.wait_ge(out_sent, at1(b, 16 * G, 0))
                blocks = slice(2 * t, 2 * t + 2)
                dve.wait_ge(full["acc"], at(b, 8, 4 * pair + t + 1))
                src = side.rearrange("p (i d) -> p i d", i=2)
                into = x_mid if pair else x_acc
                nc.vector.tensor_tensor(into[:, blocks, :], src, x_acc[:, blocks, :], ALU.add).then_inc(taken["acc"], 1)
                if pair:
                    if t == 3:
                        dve.drain().then_inc(x_acc_used, 1)
                    else:
                        settle()
                    block_stats(x_mid, t)

            def t2_tile(b, t, side=side):
                dve.wait_ge(full["t2"], at(b, 4, t + 1))
                nc.vector.tensor_copy(xn2t[:, :, 2 * t * P:(2 * t + 2) * P], side.rearrange("p (k n) -> p k n", k=KC)
                                      ).then_inc(taken["t2"], 1)
                if t < 2:
                    layernorm(x_mid, 1, t + 2, xn2_ready)

            def route_tile(b, t, side=side):
                dve.wait_ge(full["route"], at(b, TILES["route"], t + 1))
                if t == 0:
                    nc.vector.tensor_copy(logits_t[:, :], side[:, 0:2 * P]).then_inc(taken["route"], 1)
                elif t == 1:
                    nc.vector.tensor_copy(logits[:, :, :].rearrange("p (j i) e -> p i j e", i=2),
                                          side[:, 0:2 * P].rearrange("p (i j e) -> p i j e", i=2, j=4)[:, :, :, 0:E]
                                          ).then_inc(taken["route"], 1)
                else:
                    nc.vector.tensor_reduce(routed[:, :], side[0:1, 0:NB], AXIS_X, ALU.add).then_inc(taken["route"], 1)
                    settle()
                    nc.vector.tensor_copy(routed_i[:, :], routed[:, :]).then_inc(routed_ready, 1)
                if t == 1:
                    settle()
                    for i in range(NB):
                        nc.vector.max(top[:, i, :], logits[:, i, :])
                    settle()
                    nc.vector.tensor_tensor(gap[:, :], top[:, :, 1], top[:, :, 0], ALU.subtract).then_inc(gap_ready, 1)

            def route(b):
                dve.wait_ge(gap_exped, at(b, 1, 1))
                nc.vector.tensor_scalar(weight[:, :], gap_exp[:, :], 1.0, None, ALU.add)
                settle()
                nc.vector.reciprocal(weight[:, :], weight[:, :])
                settle()
                nc.vector.tensor_scalar(weight[:, :], weight[:, :], 1.0, None, ALU.is_ge).then_inc(weight_ready, 1)

            def ffn_tile(b, t, side=side):
                what, pair = FFN[t]
                dve.wait_ge(full["ffn"], at(b, TILES["ffn"], t + 1))
                if what == "up":
                    h = hidden2[:, pair % 2, :]
                    nc.vector.tensor_scalar(h, side[:, 0:2 * P], 0.0, None, ALU.max).then_inc(taken["ffn"], 1)
                    settle()
                    nc.vector.tensor_tensor(h, h, h, ALU.mult).then_inc(hidden_ready, 1)
                else:
                    y = x_mid[:, 2 * pair:2 * pair + 2, :]
                    nc.vector.tensor_tensor(y, side.rearrange("p (i d) -> p i d", i=2), y, ALU.add
                                            ).then_inc(taken["ffn"], 1)
                    dve.drain().then_inc(out_ready, 1)

            def experts(b):
                dve.wait_ge(routed_ready, at(b, 1, 1))
                dve.sem_inc(held["dve"], 1)
                count = dve.value_load(routed_i[0:1, 0:1], min_val=0, max_val=C)
                with dve.If(count > 0):
                    for i in range(NB):
                        nc.vector.tensor_scalar(prob[:, i, :], logits[:, i, :], top[:, i, 0:1], weight[:, i:i + 1],
                                                ALU.is_equal, ALU.mult)
                    settle()
                    with dve.Fori(0, E) as e:
                        base = at(b, TILES["gen"], 0) + e * 12
                        for pair in range(4):
                            for i in range(2):
                                last = nc.vector.tensor_copy(gate[:, i * P:(i + 1) * P],
                                                             prob[:, 2 * pair + i, bass.ds(e, 1)].to_broadcast([P, P]))
                            last.then_inc(gate_ready, 1)
                            settle()
                            dve.wait_ge(full["gen"], base + (3 * pair + 1))
                            nc.vector.tensor_copy(gate[:, :], side[:, 0:2 * P]).then_inc(taken["gen"], 1)
                            settle()
                            dve.wait_ge(full["gen"], base + (3 * pair + 2))
                            nc.vector.scalar_tensor_tensor(hidden2[:, 0, :], side[:, 0:2 * P], 0.0, gate[:, :], ALU.max, ALU.mult)
                            settle()
                            nc.vector.tensor_tensor(hidden[:, :], hidden2[:, 0, :], hidden2[:, 0, :], ALU.mult
                                                    ).then_inc(taken["gen"], 1)
                            dve.wait_ge(full["gen"], base + (3 * pair + 3))
                            x = x_mid[:, 2 * pair:2 * pair + 2, :]
                            nc.vector.tensor_tensor(x, side.rearrange("p (i d) -> p i d", i=2), x, ALU.add
                                                    ).then_inc(taken["gen"], 1)
                            settle()
                with dve.Else():
                    dve.sem_inc(taken["gen"], TILES["gen"])
                    dve.sem_inc(gate_ready, 4 * E)
                settle()

            def batch(b, first, last):
                for g in range(G):
                    b0, g0 = (b, g - 1) if g else (b - 1, G - 1)
                    for s in range(NSTEP):
                        kind, t = SIDE[g].get(s, ("none", 0))
                        if not runs(kind, g, first, last):
                            kind = "none"
                        if kind == "norm" and t == 0:
                            if g == 2:
                                reciprocals(b0, g0)
                            spread_reciprocals(at(b, 16, 12 if g == 1 else 16))
                        if s == RECIPROCALS and g != 2 and not (first and g == 0):
                            reciprocals(b0, g0)
                        if (g, s) == STATS2 and not first:
                            layernorm_stats(1)
                            for t0 in range(2):
                                layernorm(x_mid, 1, t0, xn2_ready)
                        if (g, s) in STATS1 and not last:
                            t0 = STATS1[g, s]
                            if t0 == 0:
                                dve.wait_ge(x_loaded, at(b, 16, 32))
                            if t0 < 4:
                                block_stats(x_in, t0)
                            else:
                                layernorm_stats(0)
                                for t0 in range(2):
                                    layernorm(x_in, 0, t0, xn_ready)
                        if s == TAKE_Y[g]:
                            take_y(b, g, 0)
                        if kind == "v":
                            v_tile(b, first, t)
                        elif kind == "xt":
                            xt_tile(b + 1, t)
                        elif kind == "qk":
                            b1, g1 = (b, g + 1) if g < G - 1 else (b + 1, 0)
                            qk_tile(b1, g1, t, False)
                        elif kind == "norm":
                            norm_tile(b - PAIR_OF[g], PAIR_OF[g], t)
                        elif kind == "acc":
                            acc_tile(b - PAIR_OF[g], PAIR_OF[g], t)
                        elif kind == "t2":
                            t2_tile(b - 1, t)
                        elif kind == "route":
                            if t == 2:
                                route(b - 1)
                            route_tile(b - 1, t)
                        elif kind == "ffn":
                            ffn_tile(b - 1, t)
                        if (g, s) == BRANCH and not first:
                            experts(b - 1)
                    take_y(b, g, 1)

            dve.sem_inc(taken["ffn"], 1)
            dve.sem_inc(taken["gen"], 1)
            dve.wait_ge(x_loaded, 16)
            for t in range(4):
                block_stats(x_in, t)
            layernorm_stats(0)
            for t in range(2):
                layernorm(x_in, 0, t, xn_ready)
            for t in range(4):
                xt_tile(0, t, bank(t))
            dve.wait_ge(tables_loaded, 32)
            for t in range(4):
                qk_tile(0, 0, t, True, bank(4 + t))
            batch(0, True, False)
            with dve.Fori(1, B - 1) as b:
                batch(b, False, False)
            batch(B - 1, False, True)
            last_b = B - 1
            reciprocals(last_b, G - 1)
            spread_reciprocals(at(last_b, 16, 16))
            for t in range(2):
                norm_tile(last_b, 1, t, bank(t))
            for t in range(4):
                acc_tile(last_b, 1, t, bank(2 + t))
            layernorm_stats(1)
            for t in range(2):
                layernorm(x_mid, 1, t, xn2_ready)
            for t in range(4):
                t2_tile(last_b, t, bank(t))
            for n, (kind, t) in enumerate(LAST_TILES):
                if (kind, t) == ("route", 2):
                    route(last_b)
                (route_tile if kind == "route" else ffn_tile)(last_b, t, bank(n % 4))
            experts(last_b)


_INS = ['L0_attn_x', 'L0_attn_Wqkv', 'L0_attn_Wout', 'L0_attn_bout', 'L0_ffn_Ws1', 'L0_ffn_Ws2', 'L0_ffn_W1',
        'L0_ffn_W2', 'L0_ffn_Wr']


def rope_tables():
    i = np.arange(DH // 2, dtype=np.float32)
    theta = np.power(np.float32(10000.0), np.float32(-2.0) * (i - np.float32(1.0)) / np.float32(DH))
    angle = np.arange(C, dtype=np.float32)[None, :] * theta[:, None]
    d = (np.arange(P) % (DH * HG)) // HG
    sign = np.where(d % 2 == 0, np.float32(-1.0), np.float32(1.0))
    cos, sin = np.cos(angle)[d // 2], np.sin(angle)[d // 2] * sign[:, None]
    return np.ascontiguousarray(cos, np.float32), np.ascontiguousarray(sin, np.float32)


def kernel(**inputs):
    import numpy as _np
    import concourse.bacc as _bacc
    from concourse import mybir as _mybir
    from concourse.bass_utils import run_bass_kernel_spmd as _run

    nc = _bacc.Bacc("TRN2", target_bir_lowering=False, num_devices=1)
    arrays, args = {}, []
    for name in _INS:
        a = _np.ascontiguousarray(inputs[name])
        arrays[f"in_{name}"] = a
        args.append(nc.dram_tensor(f"in_{name}", a.shape, _mybir.dt.from_np(a.dtype), kind="ExternalInput").ap())
    for name, a in zip(("cos", "sin"), rope_tables()):
        arrays[f"in_{name}"] = a
        args.append(nc.dram_tensor(f"in_{name}", a.shape, _mybir.dt.from_np(a.dtype), kind="ExternalInput").ap())
    args.append(nc.dram_tensor("out_0", (B, C, D), _mybir.dt.float32, kind="ExternalOutput").ap())
    block(nc, *args)
    r = _run(nc, [arrays], core_ids=[0])
    return r.results[0]["out_0"]
```
